# Optimizing a Trainium2 kernel written in Bass

```python
import numpy as np
import jax
import jax.numpy as jnp

def _softmax(x, axis=-1):
    return jax.nn.softmax(x, axis=axis)

def _gelu(x):
    return jax.nn.gelu(x, approximate=True)

def _silu(x):
    return jax.nn.silu(x)

def _sigmoid(x):
    return jax.nn.sigmoid(x)

def _layernorm(x, axis=-1, eps=1e-05):
    m = jnp.mean(x, axis=axis, keepdims=True)
    v = jnp.var(x, axis=axis, keepdims=True)
    return (x - m) / jnp.sqrt(v + eps)

def _scatter_add(tgt, idx, src, axis=0):
    return tgt.at[idx].add(src)

def _segment_sum(src, seg, n):
    return jax.ops.segment_sum(src, seg, n)
kernel_name = 'mk_xattn_ffn_d2_seqx_r8_8b6f01'

def setup_inputs(seed: int=0):
    np.random.seed(seed)
    _w = jnp.asarray

    def _rec_inputs():
        import jax
        import jax.numpy as jnp
        _rk = jax.random.key(seed)
        x = -0.0003929 + 0.9999 * jax.random.normal(jax.random.fold_in(_rk, 1), (4, 256, 512), jnp.float32)
        _lenS = 256 - jax.random.randint(jax.random.fold_in(_rk, 7), (4,), 0, max(1, 256 // 4) + 1, jnp.int32)
        _lenS2 = 64 - jax.random.randint(jax.random.fold_in(_rk, 8), (4,), 0, max(1, 64 // 4) + 1, jnp.int32)
        _ctx_1024P = jax.random.normal(jax.random.fold_in(_rk, 11), (4, 16, 128), jnp.float32)
        _ctx_1024c = jax.random.dirichlet(jax.random.fold_in(_rk, 511), 0.3 * jnp.ones((16,), jnp.float32), (4, 64))
        _ctx_1024t = jnp.einsum('bsk,bkd->bsd', _ctx_1024c, _ctx_1024P)
        _ctx_1024t = _ctx_1024t * jax.lax.rsqrt(jnp.mean(jnp.square(_ctx_1024t)) + 1e-12) * 0.953939
        ctx_1024 = -1.39393e-06 + 0.999914 * (_ctx_1024t + 0.3 * jax.random.normal(jax.random.fold_in(_rk, 611), (4, 64, 128), jnp.float32))
        _validS = jnp.arange(256)[None, :] < _lenS[:, None]
        _validS2 = jnp.arange(64)[None, :] < _lenS2[:, None]
        _causal = jnp.tril(jnp.ones((256, 256), dtype=bool))
        mask_SxS2_ff0 = jnp.where(jnp.ones((256, 64), dtype=bool), 0.0, -1000000000.0).astype(jnp.float32)
        return (x, ctx_1024, _lenS2, mask_SxS2_ff0)
    x, ctx_1024, _lenS2, mask_SxS2_ff0 = _rec_inputs()

    def _L0_xattn_setup():
        import math
        import jax, jax.numpy as jnp
        import numpy as np
        N_HEADS = 32
        N_KV_HEADS = 8
        N_REP = N_HEADS // N_KV_HEADS
        HEAD_DIM = 512 // N_HEADS
        key = jax.random.key(seed)
        kq, kk, kv = jax.random.split(key, 3)
        B, S, T = (2, 256, 256)
        q = jax.random.normal(kq, (B, S, N_HEADS * HEAD_DIM), dtype=jnp.float32)
        k = jax.random.normal(kk, (B, T, N_KV_HEADS * HEAD_DIM), dtype=jnp.float32)
        v = jax.random.normal(kv, (B, T, N_KV_HEADS * HEAD_DIM), dtype=jnp.float32)
        mask = jnp.zeros((S, T), dtype=jnp.float32)
        return {'q': q, 'k': k, 'v': v, 'start_pos': 0, 'mask': mask}
    _L0_xattn_all = _L0_xattn_setup()
    _L0_xattn_in = {k: v for k, v in _L0_xattn_all.items() if k in ()}
    del _L0_xattn_all

    def _L0_ffn_setup():
        import jax, jax.numpy as jnp
        import numpy as np
        H = 512
        I = 1792
        G = 128

        def dequant(q, s, g=G):
            O, In = q.shape
            return (q.reshape(O, In // g, g).astype(s.dtype) * s[:, :, None]).reshape(O, In)
        key = jax.random.key(seed)
        ks = jax.random.split(key, 7)
        x = jax.random.normal(ks[0], (2, 256, H), dtype=jnp.float32)

        def mk_qlinear(kq, ksc, out_d, in_d):
            q = jax.random.randint(kq, (out_d, in_d), -8, 8, dtype=jnp.int32)
            s = jax.random.uniform(ksc, (out_d, in_d // G), dtype=jnp.float32, minval=0.005, maxval=0.02)
            return (q, s)
        gate_q, gate_s = mk_qlinear(ks[1], ks[2], I, H)
        up_q, up_s = mk_qlinear(ks[3], ks[4], I, H)
        down_q, down_s = mk_qlinear(ks[5], ks[6], H, I)
        return {'x': x, 'gate_q': gate_q, 'gate_s': gate_s, 'up_q': up_q, 'up_s': up_s, 'down_q': down_q, 'down_s': down_s}
    _L0_ffn_all = _L0_ffn_setup()
    _L0_ffn_in = {k: v for k, v in _L0_ffn_all.items() if k in ('gate_q', 'gate_s', 'up_q', 'up_s', 'down_q', 'down_s')}
    del _L0_ffn_all

    def _L1_xattn_setup():
        import jax, jax.numpy as jnp
        import numpy as np
        from jax import lax
        B, T, L, H, C = (32, 64, 128, 64, 512)
        A, FCH, K = (64, 10, 101)

        def _sig(z):
            return jnp.tanh(z * 0.5) * 0.5 + 0.5
        key = jax.random.key(seed)
        ks = jax.random.split(key, 20)
        sc = 0.02
        n = lambda k, sh: jax.random.normal(k, sh, dtype=jnp.float32) * sc
        inp = {'hbatch': jax.random.normal(ks[0], (B, T, 2 * H), dtype=jnp.float32), 'targets': jax.random.normal(ks[1], (B, L, C), dtype=jnp.float32), 'L_sy': n(ks[2], (H, H)), 'L_gy_w': n(ks[3], (H, 2 * H)), 'L_gy_b': jnp.zeros((H,), jnp.float32), 'L_yy_w': n(ks[4], (C, H)), 'L_yy_b': jnp.zeros((C,), jnp.float32), 'L_ys': n(ks[5], (4 * H, C)), 'L_ss': n(ks[6], (4 * H, H)), 'L_gs_w': n(ks[7], (4 * H, 2 * H)), 'L_gs_b': jnp.zeros((4 * H,), jnp.float32), 'Wa_s': n(ks[8], (A, H)), 'Wa_h': n(ks[9], (A, 2 * H)), 'ba': jnp.zeros((A,), jnp.float32), 'conv_w': n(ks[10], (FCH, 1, K)), 'Wa_f': n(ks[11], (A, FCH)), 'va': n(ks[12], (A,)), 'lengths': jax.random.randint(ks[13], (B,), T // 2, T + 1)}
        return inp
    _L1_xattn_all = _L1_xattn_setup()
    _L1_xattn_in = {k: v for k, v in _L1_xattn_all.items() if k in ('L_sy', 'L_gy_w', 'L_gy_b', 'L_yy_w', 'L_yy_b', 'L_ys', 'L_ss', 'L_gs_w', 'L_gs_b', 'Wa_s', 'Wa_h', 'ba', 'conv_w', 'Wa_f', 'va')}
    del _L1_xattn_all

    def _L1_ffn_setup():
        import jax, jax.numpy as jnp
        import numpy as np
        NUM_EXPERTS = 16
        TOP_K = 2
        INTER = 56
        key = jax.random.key(seed)
        k1, k2, k3, k4, k5 = jax.random.split(key, 5)
        B, S, H = (4, 256, 512)
        scale = 0.02
        return {'hid': jax.random.normal(k1, (B, S, H), dtype=jnp.float32), 'gate_w': jax.random.normal(k2, (NUM_EXPERTS, H), dtype=jnp.float32) * scale, 'u': jax.random.normal(k3, (NUM_EXPERTS * INTER, H), dtype=jnp.float32) * scale, 'g': jax.random.normal(k4, (NUM_EXPERTS * INTER, H), dtype=jnp.float32) * scale, 'd': jax.random.normal(k5, (H, NUM_EXPERTS * INTER), dtype=jnp.float32) * scale}
    _L1_ffn_all = _L1_ffn_setup()
    _L1_ffn_in = {k: v for k, v in _L1_ffn_all.items() if k in ('gate_w', 'u', 'g', 'd')}
    del _L1_ffn_all
    return {'x': x, 'ctx_1024': ctx_1024, '_lenS2': _lenS2, 'mask_SxS2_ff0': mask_SxS2_ff0, 'L0_ffn_gate_q': _L0_ffn_in['gate_q'], 'L0_ffn_gate_s': _L0_ffn_in['gate_s'], 'L0_ffn_up_q': _L0_ffn_in['up_q'], 'L0_ffn_up_s': _L0_ffn_in['up_s'], 'L0_ffn_down_q': _L0_ffn_in['down_q'], 'L0_ffn_down_s': _L0_ffn_in['down_s'], 'L1_xattn_L_sy': _L1_xattn_in['L_sy'], 'L1_xattn_L_gy_w': _L1_xattn_in['L_gy_w'], 'L1_xattn_L_gy_b': _L1_xattn_in['L_gy_b'], 'L1_xattn_L_yy_w': _L1_xattn_in['L_yy_w'], 'L1_xattn_L_yy_b': _L1_xattn_in['L_yy_b'], 'L1_xattn_L_ys': _L1_xattn_in['L_ys'], 'L1_xattn_L_ss': _L1_xattn_in['L_ss'], 'L1_xattn_L_gs_w': _L1_xattn_in['L_gs_w'], 'L1_xattn_L_gs_b': _L1_xattn_in['L_gs_b'], 'L1_xattn_Wa_s': _L1_xattn_in['Wa_s'], 'L1_xattn_Wa_h': _L1_xattn_in['Wa_h'], 'L1_xattn_ba': _L1_xattn_in['ba'], 'L1_xattn_conv_w': _L1_xattn_in['conv_w'], 'L1_xattn_Wa_f': _L1_xattn_in['Wa_f'], 'L1_xattn_va': _L1_xattn_in['va'], 'L1_ffn_gate_w': _L1_ffn_in['gate_w'], 'L1_ffn_u': _L1_ffn_in['u'], 'L1_ffn_g': _L1_ffn_in['g'], 'L1_ffn_d': _L1_ffn_in['d']}

def reference(x, ctx_1024, _lenS2, mask_SxS2_ff0, L0_ffn_gate_q, L0_ffn_gate_s, L0_ffn_up_q, L0_ffn_up_s, L0_ffn_down_q, L0_ffn_down_s, L1_xattn_L_sy, L1_xattn_L_gy_w, L1_xattn_L_gy_b, L1_xattn_L_yy_w, L1_xattn_L_yy_b, L1_xattn_L_ys, L1_xattn_L_ss, L1_xattn_L_gs_w, L1_xattn_L_gs_b, L1_xattn_Wa_s, L1_xattn_Wa_h, L1_xattn_ba, L1_xattn_conv_w, L1_xattn_Wa_f, L1_xattn_va, L1_ffn_gate_w, L1_ffn_u, L1_ffn_g, L1_ffn_d):
    import jax
    import jax.numpy as jnp

    def _L0_xattn_ref(q, k, v, start_pos, mask):
        import math
        import jax, jax.numpy as jnp
        import numpy as np
        N_HEADS = 32
        N_KV_HEADS = 8
        N_REP = N_HEADS // N_KV_HEADS
        HEAD_DIM = 512 // N_HEADS
        b, s, _ = q.shape
        t = k.shape[1]
        xq = q.reshape(b, s, N_KV_HEADS, N_REP, HEAD_DIM)
        xk = k.reshape(b, t, N_KV_HEADS, HEAD_DIM)
        xv = v.reshape(b, t, N_KV_HEADS, HEAD_DIM)
        scores = jnp.einsum('bsgrd,btgd->bgrst', xq, xk) / math.sqrt(HEAD_DIM)
        scores = scores + mask
        probs = jax.nn.softmax(scores.astype(jnp.float32), axis=-1).astype(q.dtype)
        out = jnp.einsum('bgrst,btgd->bsgrd', probs, xv)
        return out.reshape(b, s, N_HEADS * HEAD_DIM)

    def _L0_ffn_ref(x, gate_q, gate_s, up_q, up_s, down_q, down_s):
        import jax, jax.numpy as jnp
        import numpy as np
        H = 512
        I = 1792
        G = 128

        def dequant(q, s, g=G):
            O, In = q.shape
            return (q.reshape(O, In // g, g).astype(s.dtype) * s[:, :, None]).reshape(O, In)
        Wg = dequant(gate_q, gate_s)
        Wu = dequant(up_q, up_s)
        Wd = dequant(down_q, down_s)
        gate_score = jax.nn.silu(jnp.einsum('bsh,ih->bsi', x, Wg))
        intermediate = gate_score * jnp.einsum('bsh,ih->bsi', x, Wu)
        return jnp.einsum('bsi,hi->bsh', intermediate, Wd)

    def _L1_xattn_ref(hbatch, targets, L_sy, L_gy_w, L_gy_b, L_yy_w, L_yy_b, L_ys, L_ss, L_gs_w, L_gs_b, Wa_s, Wa_h, ba, conv_w, Wa_f, va, lengths):
        import jax, jax.numpy as jnp
        import numpy as np
        from jax import lax
        B, T, L, H, C = (32, 64, 128, 64, 512)
        A, FCH, K = (64, 10, 101)

        def _sig(z):
            return jnp.tanh(z * 0.5) * 0.5 + 0.5
        Bx, Tx, D = hbatch.shape
        mask = jnp.arange(Tx)[None, :] < lengths[:, None]
        enc_proj = jnp.einsum('btd,ad->bta', hbatch, Wa_h)

        def step(carry, tgt):
            s, c, alpha = carry
            f = lax.conv_general_dilated(alpha, conv_w, (1,), 'SAME', dimension_numbers=('NCH', 'OIH', 'NCH'))
            e = jnp.einsum('a,bta->bt', va, jnp.tanh(enc_proj + (s @ Wa_s.T)[:, None, :] + jnp.einsum('bft,af->bta', f, Wa_f) + ba))
            e = jnp.where(mask, e, jnp.float32(-1e+30))
            alpha_new = jax.nn.softmax(e, axis=1)[:, None, :]
            g = jnp.einsum('bt,btd->bd', alpha_new[:, 0], hbatch)
            y = jnp.tanh(g @ L_gy_w.T + L_gy_b + s @ L_sy.T) @ L_yy_w.T + L_yy_b
            rec = tgt @ L_ys.T + s @ L_ss.T + g @ L_gs_w.T + L_gs_b
            ig, fg, cg, og = jnp.split(rec, 4, axis=1)
            c_next = _sig(fg) * c + _sig(ig) * jnp.tanh(cg)
            s_next = _sig(og) * jnp.tanh(c_next)
            return ((s_next, c_next, alpha_new), y)
        init = (jnp.zeros((Bx, L_sy.shape[0]), hbatch.dtype), jnp.zeros((Bx, L_sy.shape[0]), hbatch.dtype), jnp.zeros((Bx, 1, Tx), hbatch.dtype))
        _, ys = lax.scan(step, init, jnp.swapaxes(targets, 0, 1))
        return jnp.swapaxes(ys, 0, 1)

    def _L1_ffn_ref(hid, gate_w, u, g, d):
        import jax, jax.numpy as jnp
        import numpy as np
        NUM_EXPERTS = 16
        TOP_K = 2
        INTER = 56
        B, S, H = hid.shape
        x = hid.reshape(-1, H)
        bs = x.shape[0]
        logits = x @ gate_w.T
        probs = jax.nn.softmax(logits.astype(jnp.float32), axis=-1)
        vals, idx = jax.lax.top_k(probs, TOP_K)
        vals = vals / jnp.sum(vals, axis=-1, keepdims=True)
        rows = jnp.arange(bs)[:, None]
        w = jnp.zeros((bs, NUM_EXPERTS), dtype=jnp.float32).at[rows, idx].set(vals)
        w = w.astype(x.dtype)
        gate_out = (x @ g.T).reshape(bs, NUM_EXPERTS, INTER)
        up_out = (x @ u.T).reshape(bs, NUM_EXPERTS, INTER)
        h = jax.nn.silu(gate_out) * up_out
        d_r = d.reshape(H, NUM_EXPERTS, INTER)
        out = jnp.einsum('bei,hei,be->bh', h, d_r, w)
        return out.reshape(B, S, H)
    x = x + _L0_xattn_ref(_layernorm(x, axis=-1), ctx_1024, ctx_1024, 0, mask_SxS2_ff0)
    x = x + _L0_ffn_ref(_layernorm(x, axis=-1), L0_ffn_gate_q, L0_ffn_gate_s, L0_ffn_up_q, L0_ffn_up_s, L0_ffn_down_q, L0_ffn_down_s)
    x = x + _L1_xattn_ref(ctx_1024, _layernorm(x, axis=-1), L1_xattn_L_sy, L1_xattn_L_gy_w, L1_xattn_L_gy_b, L1_xattn_L_yy_w, L1_xattn_L_yy_b, L1_xattn_L_ys, L1_xattn_L_ss, L1_xattn_L_gs_w, L1_xattn_L_gs_b, L1_xattn_Wa_s, L1_xattn_Wa_h, L1_xattn_ba, L1_xattn_conv_w, L1_xattn_Wa_f, L1_xattn_va, _lenS2)
    x = x + _L1_ffn_ref(_layernorm(x, axis=-1), L1_ffn_gate_w, L1_ffn_u, L1_ffn_g, L1_ffn_d)
    return x

_drawn_inputs = setup_inputs


def setup_inputs(seed=0):
    import zlib

    import numpy as np

    out = dict(_drawn_inputs(seed))
    spreads = {'mask_SxS2_ff0': (0.0, 0.474),
     'L1_xattn_L_gy_b': (0.0, 0.8),
     'L1_xattn_L_yy_b': (0.0, 0.292),
     'L1_xattn_L_gs_b': (0.0, 0.8),
     'L1_xattn_ba': (0.0, 0.8)}
    factors = {'L1_xattn_L_sy': 8.0,
     'L1_xattn_L_gy_w': 8.0,
     'L1_xattn_L_yy_w': 7.746,
     'L1_xattn_L_ys': 8.0,
     'L1_xattn_L_ss': 8.0,
     'L1_xattn_L_gs_w': 8.0,
     'L1_xattn_Wa_s': 8.0,
     'L1_xattn_Wa_h': 8.0,
     'L1_xattn_conv_w': 23.55,
     'L1_xattn_Wa_f': 8.0,
     'L1_xattn_va': 8.0,
     'L1_ffn_gate_w': 8.0,
     'L1_ffn_u': 8.0,
     'L1_ffn_g': 8.0,
     'L1_ffn_d': 8.0}
    for name, (base, spread) in spreads.items():
        noise = np.random.default_rng([zlib.crc32(name.encode()), seed]).standard_normal(out[name].shape)
        drawn = base * np.exp(spread * noise) if base else spread * noise
        out[name] = jnp.asarray(drawn.astype(out[name].dtype))
    for name, factor in factors.items():
        out[name] = (out[name] * factor).astype(out[name].dtype)
    return out
```

```python
from contextlib import ExitStack

import numpy as np

import concourse.bass as bass
from concourse import mybir

ALU = mybir.AluOpType
ACT = mybir.ActivationFunctionType
F32 = mybir.dt.float32
BF16 = mybir.dt.bfloat16
I32 = mybir.dt.int32
U32 = mybir.dt.uint32
AX = mybir.AxisListType

P = 128
B, S, H = 4, 256, 512
T, D = 64, 128
NCH = 2
CL = S // NCH
KT = H // P
HEADS, HD = 32, 16
I0, IT0 = 1792, 14
NE, EI = 16, 56
I1, IT1 = NE * EI, NE * EI // P
J = 64
KW = 101
FCH = 10
NF = 128
BIG = 1.0e30
EPS = 1e-5


def shape_constants():
    t = np.arange(T)
    kap = np.arange(KW) - KW // 2
    fwd = np.zeros((2 * P, T), np.float64)
    inv = np.zeros((2 * P, T), np.float64)
    ker = np.zeros((2 * P, KW), np.float64)
    r = 0
    for m in range(NF // 2 + 1):
        w = 2 * np.pi * m / NF
        edge = m in (0, NF // 2)
        c = (1.0 if edge else 2.0) / NF
        cos, sin = np.cos, np.sin
        for fa, fb, fc, sign in ((cos, cos, cos, 1), (cos, sin, sin, -1), (sin, sin, cos, 1), (sin, cos, sin, 1)):
            fwd[r], inv[r], ker[r] = fa(w * t), fb(w * t), sign * c * fc(w * kap)
            r += 1
            if edge:
                break
    f32 = np.float32
    bl = np.arange(P) // T
    return {
        "c_ident": np.eye(P, dtype=f32),
        "c_fwd": np.stack([np.tile(fwd[q * P:(q + 1) * P].T, (2, 1)) for q in range(2)], 1).astype(f32),
        "c_inv": np.stack([inv[q * P:(q + 1) * P] for q in range(2)], 1).astype(f32),
        "c_ker": np.stack([ker[q * P:(q + 1) * P].T for q in range(2)], 1).astype(f32),
        "c_headsel": (np.arange(P)[:, None] // HD == np.arange(8)[None]).astype(f32),
        "c_expert": (np.arange(I1)[None] // EI == np.arange(NE)[:, None]).astype(f32),
        "c_iota": np.tile(np.arange(NE, dtype=f32), (P, 1)),
        "c_tvec": np.tile(np.arange(T, dtype=f32), B)[None],
        "c_gatescale": np.stack([np.where(np.arange(P) < J, 1.0, 2.0), np.ones(P)], 1).astype(f32),
        "c_selrow": np.stack([np.ones(P), bl == 0, bl == 1]).astype(f32),
        "c_offdiag": np.stack([np.tile(np.repeat([0, 1], T), 2), np.tile(np.repeat([1, 0], T), 2)]).astype(f32) * (2 * BIG),
    }


def build(nc, a, out):
    with ExitStack() as ctx:
        def sb(name, shape, dt=F32):
            return ctx.enter_context(nc.sbuf_tensor(name, shape, dt))

        def sem(name):
            return ctx.enter_context(nc.semaphore(name))

        x_sb = sb("x_sb", [P, NCH * B, H])
        xn = sb("xn", [P, 2, H])
        xT = sb("xT", [P, KT, B * CL])
        stats = sb("stats", [P, 2, 6])
        mv = sb("mv", [P, 2, 2])
        rstd = sb("rstd", [P, 2, 1])
        vareps = sb("vareps", [P, 1])
        minus_half = sb("minus_half", [P, 1])
        krep = sb("krep", [P, KT, B, T])
        headsel = sb("headsel", [P, 8])
        kbd = sb("kbd", [P, 2, 512])
        vbd = sb("vbd", [P, B, 8, 34])
        mask_sb = sb("mask_sb", [P, NCH, T])
        smax = sb("smax", [P, 32])
        rsum = sb("rsum", [P, HEADS])
        wbig = sb("wbig", [P, 2 * KT * I0 + IT0 * H])
        sscale = sb("sscale", [P, 2, I0])
        interT = sb("interT", [P, IT0, B * CL])
        sc = interT[:, 0:4, :]
        pT = interT[:, 4:6, :]
        tanh_sb = sb("tanh_sb", [P, 2, 512])
        act_sb = sb("act_sb", [P, 2, 512])
        otmp = act_sb[:, 0, :]
        lys = sb("lys", [P, KT, 256])
        gbias = sb("gbias", [P, 2])
        gscale = sb("gscale", [P, 2])
        rin = sb("rin", [P, S, 8])
        ident = sb("ident", [P, P])
        ctxT = sb("ctxT", [P, 2, P])
        wahT = sb("wahT", [P, J])
        ba2 = sb("ba2", [P, 1])
        lgsT = sb("lgsT", [P, 256])
        lgyT = sb("lgyT", [P, J])
        lssT = sb("lssT", [J, 256])
        lsyT = sb("lsyT", [J, J])
        wasT = sb("wasT", [J, 2, P])
        convw = sb("convw", [FCH, KW])
        wafT = sb("wafT", [FCH, J])
        va2 = sb("va2", [P, 1])
        vab = sb("vab", [P, 2, P])
        fwd = sb("fwd", [P, 2, P])
        inv = sb("inv", [P, 2, T])
        ker = sb("ker", [KW, 2, P])
        u_sb = sb("u_sb", [KW, J])
        uh = sb("uh", [P, 2, J])
        enc = sb("enc", [P, P])
        hg = sb("hg", [P, 2, 256])
        hy = sb("hy", [P, 2, J])
        ones = sb("ones", [P, P])
        tvec = sb("tvec", [1, B * T])
        leni = sb("leni", [1, B], I32)
        lenf = sb("lenf", [1, B])
        selrow_f = sb("selrow_f", [3, P])
        maskrhs_f = sb("maskrhs_f", [3, B * T])
        selrow = sb("selrow", [3, P], BF16)
        maskrhs = sb("maskrhs", [3, B * T], BF16)
        onehot = sb("onehot", [1, 2, 2], BF16)
        bgy = sb("bgy", [J, 1])
        th = sb("th", [P, P])
        mx = sb("mx", [P, B])
        arg = sb("arg", [P, B])
        ex = sb("ex", [P, 2, B])
        rinv = sb("rinv", [P, 2, B])
        g1 = sb("g1", [P, 8])
        gat = sb("gat", [P, 8])
        rs = sb("rs", [P, 8])
        ahn = sb("ahn", [P, 8])
        qv = krep[:, 0:2, :, :]
        tfi = sb("tfi", [J, 8])
        xs = sb("xs", [J, 2, 12])
        ab = sb("ab", [J, 8])
        tc_sb = sb("tc_sb", [J, B])
        s2 = sb("s2", [J, 2, B])
        gwT = sb("gwT", [P, KT, NE])
        probs = sb("probs", [P, 2, NE])
        top8 = sb("top8", [P, 2, 8])
        idx8 = sb("idx8", [P, 2, 8], U32)
        idxf = sb("idxf", [P, 2, 2])
        small = sb("small", [P, 2, 4])
        wsel = sb("wsel", [P, 2, 2, NE])
        iota = sb("iota", [P, NE])

        reuse = sscale[:].rearrange("p a b -> p (a b)")
        ahist = reuse[:, 0:S * B].rearrange("p (l b) -> p l b", b=B)
        shist = reuse[0:J, S * B:2 * S * B].rearrange("p (l b) -> p l b", b=B)
        uT = reuse[0:J + 1, 2 * S * B:2 * S * B + B * CL].rearrange("p (b l) -> p b l", b=B)

        wT = reuse[0:NE, 2 * S * B + B * CL:2 * S * B + 2 * B * CL]

        ahist2 = ahist.rearrange("p (i two) b -> p i two b", two=2)
        shist2 = shist.rearrange("p (i two) b -> p i two b", two=2)
        rin2 = rin[:].rearrange("p (i two) b -> p i two b", two=2)

        bank = [ctx.enter_context(nc.psum_tensor(f"bank{i}", [P, 512], F32)) for i in range(8)]

        nw = KT * I0
        wg = wbig[:, 0:nw].rearrange("p (k o) -> p k o", k=KT)
        wu = wbig[:, nw:2 * nw].rearrange("p (k o) -> p k o", k=KT)
        wd = wbig[:, 2 * nw:].rearrange("p (k o) -> p k o", k=IT0)
        m1 = KT * I1
        w1g = wbig[:, 0:m1].rearrange("p (k o) -> p k o", k=KT)
        w1u = wbig[:, m1:2 * m1].rearrange("p (k o) -> p k o", k=KT)
        w1d = wbig[:, 2 * m1:2 * m1 + IT1 * H].rearrange("p (k o) -> p k o", k=IT1)

        lyy = wbig[0:J + 1, 3 * m1 + I1:3 * m1 + I1 + H]
        expert = wbig[0:NE, 3 * m1:3 * m1 + I1]

        names = """frame_zero vareps_ready mv_ready rstd_ready x_in attn_in w0_in sc_in rec_in setup_in w1_in fin_in out_done
            gdeq_in ln_ready tr_done xT_ready chain pchain achain
            kbd_ready score_done score_read sub_done exp_done pt_done pt_copied av_done attn_done
            deq0 deq1 gu_done th_done inter_done down_done x_added
            rec_done rin_ready
            vbd_zero setup_v setup_mm setup_ps setup_cp setup_a mask_ready scale_ready
            pre_done th_s eb_done et_done mx_read arg_ready ex_ready sum_done hg_done ah_done ahn_ready
            qd_ready qp_ready sp_done rs_done g_ready tg_ready c_ready tc_ready s_ready rinv_ready hist_done
            y_done u_ready yy_done lg_done lgx_ready pe_exp wsel_ready wt_done wT_ready""".split()
        s = {n: sem("s_" + n) for n in names}
        w_sc = [sem(f"s_scl{i}") for i in range(2)]
        w_in = [sem(f"s_w{i}") for i in range(3)]
        x_in = [sem(f"s_x{i}") for i in range(2)]

        block = ctx.enter_context(nc.Block())
        NSC = 9
        DPART = [(0, 3), (3, 6), (6, 9), (9, 12), (12, 14)]

        @block.sync
        def _(sp):
            for c in range(NCH):
                sp.dma_start(x_sb[:, c * B:(c + 1) * B, :], a["x"][:, c * CL:(c + 1) * CL, :].rearrange("b p h -> p b h")).then_inc(x_in[c], 16)
                if c == 0:
                    sp.dma_start(ident[:], a["c_ident"]).then_inc(s["attn_in"], 16)
                    sp.dma_start(headsel[:], a["c_headsel"]).then_inc(s["attn_in"], 16)
                    sp.dma_start(krep[:], a["krep"]).then_inc(s["attn_in"], 16)
                    sp.dma_start(mask_sb[:], a["mask_SxS2_ff0"].rearrange("(c p) t -> p c t", p=P)).then_inc(s["attn_in"], 16)
                    sp.wait_ge(s["vbd_zero"], 1)
                    for b in range(B):
                        v = a["ctx_1024"][b].rearrange("t (g d) -> t g d", g=8)
                        for h in range(2):
                            sp.dma_start(vbd[h * T:(h + 1) * T, b, :, h * 17:h * 17 + HD], v).then_inc(s["attn_in"], 16)
            for i, (dst, src) in enumerate(((wg, a["gate_qT"]), (wu, a["up_qT"]), (wd, a["down_qT"]))):
                sp.dma_start(dst.bitcast(I32), src.rearrange("(k p) o -> p k o", p=P)).then_inc(w_in[i], 16)
            for n in range(8 + len(DPART)):
                if n >= 2:
                    sp.wait_ge(s["deq0"], n - 1)
                if n < 8:
                    src = a["gate_sT"] if n < 4 else a["up_sT"]
                    sp.dma_start(sscale[:, n % 2, :], src[n % 4:n % 4 + 1, :].partition_broadcast(P)).then_inc(w_sc[n % 2], 16)
                else:
                    i0, i1 = DPART[n - 8]
                    sp.dma_start(sscale[:, n % 2, 0:(i1 - i0) * H],
                                 a["down_sT"][i0:i1, :].rearrange("g h -> (g h)").unsqueeze(0).partition_broadcast(P)).then_inc(w_sc[n % 2], 16)
            sp.dma_start(lys[:], a["LysT"].rearrange("(k p) o -> p k o", p=P)).then_inc(s["rec_in"], 16)
            sp.dma_start(gbias[:], a["gsb2"]).then_inc(s["rec_in"], 16)
            sp.dma_start(gscale[:], a["c_gatescale"]).then_inc(s["rec_in"], 16)
            sp.wait_ge(s["frame_zero"], 1)
            small_loads = [(ctxT[:], a["ctxT"]), (wahT[:], a["WahT"]), (lgsT[:], a["LgsT"]), (lgyT[:], a["LgyT"]),
                           (lssT[:], a["LssT"]), (lsyT[:], a["LsyT"]), (wasT[:, 0, 0:J], a["WasT"]), (wasT[:, 1, J:P], a["WasT"]), (convw[:], a["convw"]),
                           (wafT[:], a["WafT"]), (fwd[:], a["c_fwd"]), (inv[:], a["c_inv"]), (ker[:], a["c_ker"]),
                           (tvec[:], a["c_tvec"]), (leni[:], a["lens"]), (selrow_f[:], a["c_selrow"]),
                           (maskrhs_f[1:3, :], a["c_offdiag"])]
            for h in range(2):
                small_loads.append((ba2[h * J:(h + 1) * J, :], a["ba"]))
                small_loads.append((va2[h * J:(h + 1) * J, :], a["va"]))
            assert len(small_loads) == 21
            for dst, src in small_loads:
                sp.dma_start(dst, src).then_inc(s["setup_in"], 16)
            for dst, src in ((bgy[:], a["bgy"]), (gwT[:], a["gwT"].rearrange("(k p) e -> p k e", p=P)), (iota[:], a["c_iota"])):
                sp.dma_start(dst, src).then_inc(s["fin_in"], 16)
            sp.wait_ge(s["down_done"], 2 * B)
            for dst, src in ((w1g, a["g1T"]), (w1u, a["u1T"]), (w1d, a["d1T"])):
                sp.dma_start(dst, src.rearrange("(k p) o -> p k o", p=P)).then_inc(s["w1_in"], 16)
            for dst, src in ((expert, a["c_expert"]), (lyy[0:J, :], a["LyyT"]), (lyy[J:J + 1, :], a["byy"])):
                sp.dma_start(dst, src).then_inc(s["w1_in"], 16)
            for k in range(NCH * B):
                c, b = divmod(k, B)
                sp.wait_ge(s["x_added"], 2 * B + 2 * B * c + B + b + 1)
                sp.dma_start(out[b, c * CL:(c + 1) * CL, :], x_sb[:, k, :]).then_inc(s["out_done"], 16)
            sp.wait_ge(s["out_done"], 16 * NCH * B)

        @block.gpsimd
        def _(pool):
            nc.gpsimd.memset(vbd[:], 0.0).then_inc(s["pchain"], 1)
            nc.gpsimd.memset(wasT[:], 0.0).then_inc(s["frame_zero"], 1)
            nc.gpsimd.memset(ones[:], 1.0)
            nc.gpsimd.memset(minus_half[:], -0.5)
            pool.wait_ge(s["pchain"], 1)
            nc.gpsimd.memset(vbd[0:T, :, :, 16:17], 1.0).then_inc(s["pchain"], 1)
            pool.wait_ge(s["pchain"], 2)
            nc.gpsimd.memset(vbd[T:P, :, :, 33:34], 1.0).then_inc(s["vbd_zero"], 1)
            def rstd_of(n):
                pool.wait_ge(s["mv_ready"], n + 1)
                nc.gpsimd.tensor_scalar(vareps[:], mv[:, n % 2, 1:2], EPS, None, ALU.add).then_inc(s["vareps_ready"], 1)
                pool.wait_ge(s["vareps_ready"], n + 1)
                nc.gpsimd.tensor_tensor(rstd[:, n % 2, :], vareps[:], minus_half[:], ALU.pow).then_inc(s["rstd_ready"], 1)

            pool.wait_ge(s["attn_in"], 16 * 12)
            for k in range(NCH * B):
                b = k % B
                rstd_of(12 * (k // B) + b)
                for kt in range(KT):
                    n = k * KT + kt
                    if n >= 2:
                        pool.wait_ge(s["score_done"], n - 1)
                    nc.gpsimd.tensor_tensor(
                        kbd[:, n % 2, :].rearrange("p (h t) -> p h t", h=8),
                        krep[:, kt, b, :].unsqueeze(1).broadcast_to([P, 8, T]),
                        headsel[:].unsqueeze(2).broadcast_to([P, 8, T]), ALU.mult).then_inc(s["kbd_ready"], 1)
                if b == B - 1:
                    for j in range(B, 3 * B):
                        rstd_of(12 * (k // B) + j)
            pool.wait_ge(s["setup_in"], 16 * 21)
            nc.gpsimd.tensor_scalar(lssT[:, 0:J], lssT[:, 0:J], 0.5, None, ALU.mult)
            nc.gpsimd.tensor_scalar(lssT[:, 2 * J:4 * J], lssT[:, 2 * J:4 * J], 0.5, None, ALU.mult)
            nc.gpsimd.tensor_scalar(lsyT[:], lsyT[:], 0.5, None, ALU.mult)
            nc.gpsimd.tensor_scalar(wasT[:], wasT[:], 0.5, None, ALU.mult)
            nc.gpsimd.tensor_scalar(lgsT[:, J:2 * J], lgsT[:, J:2 * J], 2.0, None, ALU.mult).then_inc(s["scale_ready"], 1)
            nc.gpsimd.memset(xs[:], 0.0)
            nc.gpsimd.memset(s2[:], 0.0).then_inc(s["s_ready"], 1)
            nc.gpsimd.memset(vab[:], 0.0).then_inc(s["pchain"], 1)
            pool.wait_ge(s["deq0"], 8 + len(DPART))
            pool.wait_ge(s["pchain"], 3)
            nc.gpsimd.memset(uT[J:J + 1, :, :], 1.0).then_inc(s["pchain"], 1)
            pool.wait_ge(s["pchain"], 4)
            nc.gpsimd.tensor_copy(vab[0:J, 0, :], va2[0:J, 0:1].broadcast_to([J, P])).then_inc(s["pchain"], 1)
            pool.wait_ge(s["pchain"], 5)
            nc.gpsimd.tensor_copy(vab[J:P, 1, :], va2[J:P, 0:1].broadcast_to([J, P])).then_inc(s["setup_v"], 1)
            pool.wait_ge(s["setup_v"], 1)

            with pool.Fori(0, S // 2) as i:
                for par in range(2):
                    l = i * 2 + par
                    pool.wait_ge(s["s_ready"], l + 1)
                    nc.gpsimd.tensor_copy(shist2[:, bass.ds(i, 1), par, :], s2[:, par:par + 1, :]).then_inc(s["hist_done"], 1)
                    pool.wait_ge(s["ahn_ready"], l + 1)
                    nc.gpsimd.tensor_tensor(qv[:, 1, :, :], inv[:, 1, :].unsqueeze(1).broadcast_to([P, B, T]),
                                            ahn[:, 4:8].unsqueeze(2).broadcast_to([P, B, T]), ALU.mult).then_inc(s["qp_ready"], 1)
                    nc.gpsimd.tensor_tensor(ahist2[:, bass.ds(i, 1), par, :], ex[:, par:par + 1, :], rinv[:, par:par + 1, :], ALU.mult).then_inc(s["hist_done"], 1)

            for n in range(6 * B, 8 * B):
                rstd_of(n)

        @block.vector
        def _(dve):
            chain = [0]

            def link(ins):
                chain[0] += 1
                ins.then_inc(s["chain"], 1)
                dve.wait_ge(s["chain"], chain[0])

            def layernorm(n, k):
                if n >= 2:
                    dve.wait_ge(s["tr_done"], n - 1)
                q = n % 2
                link(nc.vector.bn_stats(stats[:, q, :], x_sb[:, k, :]))
                nc.vector.bn_aggr(mv[:, q, :], stats[:, q, :]).then_inc(s["mv_ready"], 1)
                dve.wait_ge(s["rstd_ready"], n + 1)
                nc.vector.tensor_scalar(xn[:, q, :], x_sb[:, k, :], mv[:, q, 0:1], rstd[:, q, 0:1],
                                        ALU.subtract, ALU.mult).then_inc(s["ln_ready"], 1)

            def attention(k):
                c = k // B
                for kt in range(KT):
                    n = k * KT + kt
                    dve.wait_ge(s["score_done"], n + 1)
                    if kt == 0 and k > 0:
                        dve.wait_ge(s["pt_done"], 4 * k)
                    v = sc[:, kt, :].rearrange("p (h t) -> p h t", h=8)
                    link(nc.vector.scalar_tensor_tensor(
                        v, bank[2 + n % 2][:].rearrange("p (h t) -> p h t", h=8), 0.25,
                        mask_sb[:, c:c + 1, :].broadcast_to([P, 8, T]), ALU.mult, ALU.add))
                    sc_max = smax[:, kt * 8:(kt + 1) * 8]
                    ins = nc.vector.tensor_reduce(sc_max, v, AX.X, ALU.max)
                    link(ins)
                    nc.vector.tensor_tensor(v, v, sc_max.unsqueeze(2).broadcast_to([P, 8, T]), ALU.subtract).then_inc(s["sub_done"], 1)
                dve.wait_ge(s["av_done"], k + 1)
                for h in range(2):
                    o = bank[6 + h][:, 0:272].rearrange("p (h e) -> p h e", e=17)
                    r = rsum[:, 16 * h:16 * h + 16]
                    link(nc.vector.reciprocal(r.unsqueeze(2), o[:, :, 16:17]))
                    link(nc.vector.tensor_tensor(otmp[:, 256 * h:256 * h + 256].rearrange("p (h d) -> p h d", d=HD), o[:, :, 0:HD],
                                                 r.unsqueeze(2).broadcast_to([P, 16, HD]), ALU.mult))
                ins = nc.vector.tensor_tensor(x_sb[:, k, :], x_sb[:, k, :], otmp, ALU.add)
                chain[0] += 1
                ins.then_inc(s["chain"], 1)
                dve.wait_ge(s["chain"], chain[0])

            def dequantise():
                for n in range(8 + len(DPART)):
                    dve.wait_ge(w_in[min(n // 4, 2)], 16)
                    dve.wait_ge(w_sc[n % 2], 16 * (n // 2 + 1))
                    if n < 8:
                        w = (wg if n < 4 else wu)[:, n % 4, :]
                        sc_ap = sscale[:, n % 2, :]
                    else:
                        i0, i1 = DPART[n - 8]
                        w = wd[:, i0:i1, :].rearrange("p k o -> p (k o)")
                        sc_ap = sscale[:, n % 2, 0:(i1 - i0) * H]
                    nc.vector.tensor_tensor(w, w.bitcast(I32), sc_ap, ALU.mult).then_inc(s["deq0"], 1)

            def swiglu(base, tiles, expert_weights):
                for it in range(tiles):
                    n = base + it
                    dve.wait_ge(s["th_done"], n + 1)
                    if n >= 2:
                        pass
                    q = n % 2
                    link(nc.vector.scalar_tensor_tensor(act_sb[:, q, :], tanh_sb[:, q, :], 1.0, bank[2 + q][:], ALU.add, ALU.mult))
                    if expert_weights:
                        link(nc.vector.scalar_tensor_tensor(act_sb[:, q, :], act_sb[:, q, :], 0.5, bank[4 + q][:], ALU.mult, ALU.mult))
                        nc.vector.tensor_tensor(interT[:, it, :], act_sb[:, q, :], bank[q][:], ALU.mult).then_inc(s["inter_done"], 1)
                    else:
                        nc.vector.scalar_tensor_tensor(interT[:, it, :], act_sb[:, q, :], 0.5, bank[4 + q][:], ALU.mult, ALU.mult).then_inc(s["inter_done"], 1)

            added = [0]

            def add_residual(k, bk, ready, count):
                dve.wait_ge(ready, count)
                added[0] += 1
                nc.vector.tensor_tensor(x_sb[:, k, :], x_sb[:, k, :], bk[:], ALU.add).then_inc(s["x_added"], 1)
                dve.wait_ge(s["x_added"], added[0])

            for c in range(NCH):
                dve.wait_ge(x_in[c], 16)
                for b in range(B):
                    layernorm(12 * c + b, c * B + b)
                    attention(c * B + b)
                if c == 0:
                    dequantise()
                for b in range(B):
                    layernorm(12 * c + 4 + b, c * B + b)
                swiglu(c * IT0, IT0, False)
                for b in range(B):
                    add_residual(c * B + b, bank[6 + b % 2], s["down_done"], c * B + b + 1)
                    layernorm(12 * c + 8 + b, c * B + b)

            dve.wait_ge(s["setup_in"], 16 * 21)
            link(nc.vector.tensor_copy(lenf[:], leni[:]))
            link(nc.vector.tensor_tensor(tvec[:].rearrange("p (b t) -> p b t", b=B), tvec[:].rearrange("p (b t) -> p b t", b=B),
                                         lenf[:].unsqueeze(2).broadcast_to([1, B, T]), ALU.is_ge))
            link(nc.vector.tensor_scalar(maskrhs_f[0:1, :], tvec[:], -BIG, None, ALU.mult))
            nc.vector.tensor_copy(selrow[:], selrow_f[:])
            nc.vector.tensor_copy(maskrhs[:], maskrhs_f[:])
            link(nc.vector.memset(onehot[:], 0.0))
            link(nc.vector.memset(onehot[:, 0, 0:1], 1.0))
            nc.vector.memset(onehot[:, 1, 1:2], 1.0).then_inc(s["mask_ready"], 1)

            with dve.Fori(0, S // 2) as i:
                for par in range(2):
                    l = i * 2 + par
                    dve.wait_ge(s["sp_done"], l + 1)
                    nc.vector.tensor_tensor(rs[:].unsqueeze(1), bank[6][:, 0:8].unsqueeze(1), rin2[:, bass.ds(i, 1), par, :], ALU.add).then_inc(s["rs_done"], 1)
                    dve.wait_ge(s["eb_done"], l + 1)
                    nc.vector.tensor_reduce(mx[:], bank[2][:, 0:256].rearrange("p (b t) -> p b t", b=B), AX.X, ALU.max).then_inc(s["mx_read"], 1)
                    dve.wait_ge(s["et_done"], l + 1)
                    dve.wait_ge(s["mx_read"], l + 1)
                    nc.vector.tensor_tensor(arg[:].rearrange("p (h l) -> p h l", h=2), bank[3][:, 0:2].unsqueeze(2).broadcast_to([P, 2, 2]),
                                            mx[:].rearrange("p (h l) -> p h l", h=2), ALU.subtract).then_inc(s["arg_ready"], 1)
                    dve.wait_ge(s["sum_done"], l + 1)
                    nc.vector.reciprocal(rinv[:, par, :], bank[3][:, 4:8]).then_inc(s["rinv_ready"], 1)
                    dve.wait_ge(s["hg_done"], l + 1)
                    dve.wait_ge(s["rinv_ready"], l + 1)
                    nc.vector.tensor_tensor(g1[:].rearrange("p (g b) -> p g b", g=2), bank[4][:, 0:8].rearrange("p (g b) -> p g b", g=2),
                                            rinv[:, par:par + 1, :].broadcast_to([P, 2, B]), ALU.mult).then_inc(s["chain"], 1)
                    dve.wait_ge(s["chain"], 3 * l + (chain[0] + 1))
                    nc.vector.tensor_tensor(gat[:], g1[:], rs[:], ALU.add).then_inc(s["g_ready"], 1)
                    dve.wait_ge(s["ah_done"], l + 1)
                    nc.vector.tensor_tensor(ahn[:].rearrange("p (g b) -> p g b", g=2), bank[5][:, 0:8].rearrange("p (g b) -> p g b", g=2),
                                            rinv[:, par:par + 1, :].broadcast_to([P, 2, B]), ALU.mult).then_inc(s["ahn_ready"], 1)
                    dve.wait_ge(s["ahn_ready"], l + 1)
                    nc.vector.tensor_tensor(qv[:, 0, :, :], inv[:, 0, :].unsqueeze(1).broadcast_to([P, B, T]),
                                            ahn[:, 0:4].unsqueeze(2).broadcast_to([P, B, T]), ALU.mult).then_inc(s["qd_ready"], 1)
                    dve.wait_ge(s["tg_ready"], l + 1)
                    nc.vector.scalar_tensor_tensor(ab[:], tfi[:], 1.0, xs[:, par, 0:8], ALU.add, ALU.mult).then_inc(s["chain"], 1)
                    dve.wait_ge(s["chain"], 3 * l + (chain[0] + 2))
                    nc.vector.scalar_tensor_tensor(xs[:, 1 - par, 0:4], ab[:, 0:4], 0.5, ab[:, 4:8], ALU.mult, ALU.add).then_inc(s["c_ready"], 1)
                    dve.wait_ge(s["tc_ready"], l + 1)
                    nc.vector.scalar_tensor_tensor(s2[:, 1 - par, :], xs[:, par, 8:12], 1.0, tc_sb[:], ALU.add, ALU.mult).then_inc(s["s_ready"], 1)
                    nc.vector.tensor_copy(mv[0:1, 0, 0:1], mv[0:1, 0, 1:2]).then_inc(s["chain"], 1)
            chain[0] += 3 * S
            dve.wait_ge(s["chain"], chain[0])

            for c in range(NCH):
                for b in range(B):
                    k = c * B + b
                    add_residual(k, bank[6 + b % 2], s["yy_done"], k + 1)
                    layernorm(24 + k, k)
                for b in range(B):
                    k = c * B + b
                    q = k % 2
                    dve.wait_ge(s["lg_done"], k + 1)
                    link(nc.vector.tensor_reduce(small[:, q, 0:1], bank[2 + q][:, 0:NE], AX.X, ALU.max, negate=True))
                    nc.vector.tensor_copy(small[:, q, 1:2], small[:, q, 0:1]).then_inc(s["lgx_ready"], 1)
                    dve.wait_ge(s["pe_exp"], k + 1)
                    link(nc.vector.max(top8[:, q, :], probs[:, q, :]))
                    nc.vector.tensor_scalar(small[:, q, 2:3], top8[:, q, 0:1], top8[:, q, 1:2], None, ALU.add)
                    link(nc.vector.max_index(idx8[:, q, :], top8[:, q, :], probs[:, q, :]))
                    link(nc.vector.reciprocal(small[:, q, 3:4], small[:, q, 2:3]))
                    link(nc.vector.tensor_copy(idxf[:, q, :], idx8[:, q, 0:2]))
                    link(nc.vector.tensor_scalar(top8[:, q, 0:2], top8[:, q, 0:2], small[:, q, 3:4], None, ALU.mult))
                    for j in range(2):
                        ins = nc.vector.tensor_scalar(wsel[:, q, j, :], iota[:], idxf[:, q, j:j + 1], top8[:, q, j:j + 1], ALU.is_equal, ALU.mult)
                    link(ins)
                    if k >= 2:
                        dve.wait_ge(s["wt_done"], k - 1)
                    link(nc.vector.tensor_tensor(wsel[:, q, 0, :], wsel[:, q, 0, :], wsel[:, q, 1, :], ALU.add))
                    nc.vector.tensor_copy(small[:, q, 2:3], small[:, q, 3:4]).then_inc(s["wsel_ready"], 1)
                swiglu(2 * IT0 + c * IT1, IT1, True)
                for b in range(B):
                    k = c * B + b
                    add_residual(k, bank[6 + b % 2], s["down_done"], 2 * B + k + 1)

        @block.scalar
        def _(act):
            def copy_xT(n, b):
                act.wait_ge(s["tr_done"], n + 1)
                nc.scalar.activation(xT[:, :, b * CL:(b + 1) * CL], bank[n % 2][:].rearrange("p (k t) -> p k t", k=KT), ACT.Copy).then_inc(s["xT_ready"], 1)

            def attention(k):
                for kt in range(KT):
                    act.wait_ge(s["sub_done"], k * KT + kt + 1)
                    nc.scalar.activation(sc[:, kt, :], sc[:, kt, :], ACT.Exp).then_inc(s["exp_done"], 1)
                for g in range(4):
                    n = 4 * k + g
                    act.wait_ge(s["pt_done"], n + 1)
                    nc.scalar.activation(pT[:, n % 2, :], bank[4 + n % 2][:], ACT.Copy).then_inc(s["pt_copied"], 1)

            def tanh_gate(base, tiles):
                for it in range(tiles):
                    n = base + it
                    act.wait_ge(s["gu_done"], n + 1)
                    if n >= 2:
                        act.wait_ge(s["inter_done"], n - 1)
                    nc.scalar.activation(tanh_sb[:, n % 2, :], bank[2 + n % 2][:], ACT.Tanh, scale=0.5).then_inc(s["th_done"], 1)

            for c in range(NCH):
                for b in range(B):
                    copy_xT(12 * c + b, b)
                    attention(c * B + b)
                for b in range(B):
                    if b == 0:
                        act.wait_ge(s["score_done"], 16 * (c + 1))
                    copy_xT(12 * c + 4 + b, b)
                tanh_gate(c * IT0, IT0)
                for b in range(B):
                    copy_xT(12 * c + 8 + b, b)
                if c == 0:
                    act.wait_ge(s["rec_in"], 48)
                    for gp in range(2):
                        last = nc.scalar.activation(gbias[:, gp:gp + 1], gbias[:, gp:gp + 1], ACT.Copy, scale=gscale[:, gp:gp + 1])
                    last.then_inc(s["achain"], 1)
                    act.wait_ge(s["achain"], 1)
                for gp in range(2):
                    act.wait_ge(s["rec_done"], 2 * c + gp + 1)
                    nc.scalar.activation(rin[:, c * CL:(c + 1) * CL, gp * 4:gp * 4 + 4].rearrange("p l b -> p b l"),
                                         bank[4 + gp][:].rearrange("p (b l) -> p b l", b=B), ACT.Identity,
                                         bias=gbias[:, gp:gp + 1], scale=gscale[:, gp:gp + 1]).then_inc(s["rin_ready"], 1)

            act.wait_ge(s["setup_mm"], 1)
            act.wait_ge(s["setup_in"], 336)
            nc.scalar.activation(u_sb[:], bank[0][0:KW, 0:J], ACT.Copy).then_inc(s["setup_cp"], 1)
            act.wait_ge(s["setup_mm"], 2)
            nc.scalar.activation(enc[:], bank[1][:, 0:P], ACT.Identity, bias=ba2[:, 0:1])
            nc.scalar.activation(hg[:], bank[2][:].rearrange("p (h g) -> p h g", h=2), ACT.Copy)
            nc.scalar.activation(hy[:], bank[3][:, 0:P].rearrange("p (h g) -> p h g", h=2), ACT.Copy)
            nc.scalar.activation(uh[:], bank[4][:, 0:P].rearrange("p (h g) -> p h g", h=2), ACT.Copy).then_inc(s["setup_cp"], 1)

            with act.Fori(0, S // 2) as i:
                for par in range(2):
                    l = i * 2 + par
                    act.wait_ge(s["pre_done"], l + 1)
                    nc.scalar.activation(th[:], bank[par][:, 0:P], ACT.Tanh).then_inc(s["th_s"], 1)
                    act.wait_ge(s["arg_ready"], l + 1)
                    nc.scalar.activation(ex[:, par, :], arg[:], ACT.Exp).then_inc(s["ex_ready"], 1)
                    act.wait_ge(s["g_ready"], l + 1)
                    nc.scalar.activation(xs[:, par, 4:12], gat[J:P, :], ACT.Tanh, scale=0.5)
                    nc.scalar.activation(tfi[:], gat[0:J, :], ACT.Tanh, scale=0.5).then_inc(s["tg_ready"], 1)
                    act.wait_ge(s["c_ready"], l + 1)
                    nc.scalar.activation(tc_sb[:], xs[:, 1 - par, 0:4], ACT.Tanh, scale=0.5).then_inc(s["tc_ready"], 1)

            act.wait_ge(s["fin_in"], 48)
            for c in range(NCH):
                for h in range(2):
                    act.wait_ge(s["y_done"], 2 * c + h + 1)
                    if h == 0 and c > 0:
                        act.wait_ge(s["yy_done"], B * c)
                    nc.scalar.activation(uT[0:J, 2 * h:2 * h + 2, :], bank[4 + h][0:J, 0:256].rearrange("p (l b) -> p b l", b=2),
                                         ACT.Tanh, bias=bgy[:, 0:1]).then_inc(s["u_ready"], 1)
                for b in range(B):
                    if c > 0 and b == 0:
                        act.wait_ge(s["gu_done"], 2 * IT0 + c * IT1)
                    copy_xT(24 + B * c + b, b)
                for b in range(B):
                    k = c * B + b
                    q = k % 2
                    act.wait_ge(s["lgx_ready"], k + 1)
                    nc.scalar.activation(probs[:, q, :], bank[2 + q][:, 0:NE], ACT.Exp, bias=small[:, q, 1:2]).then_inc(s["pe_exp"], 1)
                    act.wait_ge(s["wt_done"], k + 1)
                    nc.scalar.activation(wT[:, b * CL:(b + 1) * CL], bank[4 + q][0:NE, 0:CL], ACT.Copy).then_inc(s["wT_ready"], 1)
                tanh_gate(2 * IT0 + c * IT1, IT1)

        @block.tensor
        def _(pe):
            mm = nc.tensor.matmul

            def transposes(n):
                pe.wait_ge(s["ln_ready"], n + 1)
                if n >= 2:
                    pe.wait_ge(s["xT_ready"], n - 1)
                for kt in range(KT):
                    last = nc.tensor.transpose(bank[n % 2][:, kt * P:(kt + 1) * P], xn[:, n % 2, kt * P:(kt + 1) * P], ident[:])
                last.then_inc(s["tr_done"], 1)

            def attention(k, n_ln):
                b = k % B
                pe.wait_ge(s["xT_ready"], n_ln + 1)
                for kt in range(KT):
                    n = k * KT + kt
                    pe.wait_ge(s["kbd_ready"], n + 1)
                    if n >= 2:
                        pe.wait_ge(s["sub_done"], n - 1)
                    mm(bank[2 + n % 2][:], xT[:, kt, b * CL:(b + 1) * CL], kbd[:, n % 2, :], start=True, stop=True).then_inc(s["score_done"], 1)
                for g in range(5):
                    if g < 4:
                        n = 4 * k + g
                        pe.wait_ge(s["exp_done"], n + 1)
                        if n >= 2:
                            pe.wait_ge(s["pt_copied"], n - 1)
                        for j in range(4):
                            last = nc.tensor.transpose(bank[4 + n % 2][:, j * P:(j + 1) * P], sc[:, g, j * P:(j + 1) * P], ident[:])
                        last.then_inc(s["pt_done"], 1)
                    if g >= 1:
                        n = 4 * k + g - 1
                        pe.wait_ge(s["pt_copied"], n + 1)
                        for j in range(4):
                            p = 4 * (g - 1) + j
                            last = mm(bank[6 + p // 8][:, (p % 8) * 34:(p % 8) * 34 + 34], pT[:, n % 2, j * P:(j + 1) * P],
                                      vbd[:, b, p // 2, :], start=True, stop=True)
                last.then_inc(s["av_done"], 1)

            def gate_up(base, tiles, g, u, weights):
                for it in range(tiles):
                    n = base + it
                    if n >= 2:
                        pe.wait_ge(s["inter_done"], n - 1)
                    if weights:
                        mm(bank[n % 2][:], expert[:, it * P:(it + 1) * P], wT[:], start=True, stop=True)
                    for w, bk in ((g, bank[2 + n % 2]), (u, bank[4 + n % 2])):
                        for kt in range(KT):
                            last = mm(bk[:], w[:, kt, it * P:(it + 1) * P], xT[:, kt, :], start=(kt == 0), stop=(kt == KT - 1))
                    last.then_inc(s["gu_done"], 1)

            added = [0]

            def down(base_inter, tiles, w, base_add):
                for b in range(B):
                    if b == 0:
                        pe.wait_ge(s["inter_done"], base_inter + tiles)
                    if b >= 2:
                        pe.wait_ge(s["x_added"], base_add + b - 1)
                    for it in range(tiles):
                        last = mm(bank[6 + b % 2][:], interT[:, it, b * CL:(b + 1) * CL], w[:, it, :], start=(it == 0), stop=(it == tiles - 1))
                    last.then_inc(s["down_done"], 1)

            pe.wait_ge(s["attn_in"], 16 * 12)
            for c in range(NCH):
                for b in range(B):
                    k = c * B + b
                    transposes(12 * c + b)
                    attention(k, 12 * c + b)
                for b in range(B):
                    transposes(12 * c + 4 + b)
                if c == 0:
                    pe.wait_ge(s["deq0"], 8 + len(DPART))
                pe.wait_ge(s["xT_ready"], 12 * c + 8)
                gate_up(c * IT0, IT0, wg, wu, False)
                down(c * IT0 + 0, IT0, wd, c * B)
                for b in range(B):
                    transposes(12 * c + 8 + b)
                pe.wait_ge(s["xT_ready"], 12 * c + 12)
                if c == 0:
                    pe.wait_ge(s["rec_in"], 48)
                for gp in range(2):
                    for kt in range(KT):
                        last = mm(bank[4 + gp][:], lys[:, kt, gp * P:(gp + 1) * P], xT[:, kt, :], start=(kt == 0), stop=(kt == KT - 1))
                    last.then_inc(s["rec_done"], 1)

            pe.wait_ge(s["setup_in"], 336)
            pe.wait_ge(s["scale_ready"], 1)
            pe.wait_ge(s["setup_v"], 1)
            pe.wait_ge(s["mask_ready"], 1)
            pe.wait_ge(s["rin_ready"], 4)
            mm(bank[0][0:KW, 0:J], convw[:], wafT[:], start=True, stop=True).then_inc(s["setup_mm"], 1)
            for h in range(2):
                mm(bank[1][h * J:(h + 1) * J, 0:P], wahT[:], ctxT[:, h, :], start=True, stop=True)
                mm(bank[2][:, h * 256:(h + 1) * 256], ctxT[:, h, :], lgsT[:], start=True, stop=True)
                mm(bank[3][:, h * J:(h + 1) * J], ctxT[:, h, :], lgyT[:], start=True, stop=True)
            pe.wait_ge(s["setup_cp"], 1)
            for h in range(2):
                last = mm(bank[4][:, h * J:(h + 1) * J], ker[:, h, :], u_sb[:], start=True, stop=True)
            last.then_inc(s["setup_mm"], 1)
            pe.wait_ge(s["setup_cp"], 2)

            def masks():
                mm(bank[2][:, 0:256], selrow[:], maskrhs[:], start=True, stop=False, skip_group_check=True)
                for h in range(2):
                    mm(bank[3][:, 0:2], maskrhs[0:1, h * P:(h + 1) * P], onehot[:, h, :], start=(h == 0), stop=False, skip_group_check=True)

            masks()
            mm(bank[0][:, 0:P], ident[:], enc[:], start=True, stop=False, skip_group_check=True)

            with pe.Fori(0, S // 2) as i:
                for par in range(2):
                    l = i * 2 + par
                    st = s2[:, par, :]
                    pe.wait_ge(s["s_ready"], l + 1)
                    for h in range(2):
                        last = mm(bank[par][:, 0:P], wasT[:, h, :], st[:, 2 * h:2 * h + 2].unsqueeze(2).broadcast_to([J, 2, T]),
                                  start=False, stop=True, skip_group_check=True)
                    last.then_inc(s["pre_done"], 1)
                    for gp in range(2):
                        last = mm(bank[6][:, 4 * gp:4 * gp + 4], lssT[:, gp * P:(gp + 1) * P], st, start=True, stop=True)
                    last.then_inc(s["sp_done"], 1)
                    mm(bank[1 - par][:, 0:P], ident[:], enc[:], start=True, stop=False, skip_group_check=True)
                    pe.wait_ge(s["th_s"], l + 1)
                    for h in range(2):
                        last = mm(bank[2][:, h * P:(h + 1) * P], vab[:, h, :], th[:], start=False, stop=True, skip_group_check=True)
                    last.then_inc(s["eb_done"], 1)
                    mm(bank[3][:, 0:2], th[:], vab[:, :, 0:1].rearrange("p h o -> p (h o)"), start=False, stop=True, skip_group_check=True).then_inc(s["et_done"], 1)
                    pe.wait_ge(s["ex_ready"], l + 1)
                    e_ap = ex[:, par, :]
                    mm(bank[3][:, 4:8], ones[:], e_ap, start=True, stop=True).then_inc(s["sum_done"], 1)
                    for gp in range(2):
                        for h in range(2):
                            last = mm(bank[4][:, gp * 4 + 2 * h:gp * 4 + 2 * h + 2], hg[:, h, gp * P:(gp + 1) * P], ex[:, par, 2 * h:2 * h + 2], start=True, stop=True)
                    last.then_inc(s["hg_done"], 1)
                    for q in range(2):
                        last = mm(bank[5][:, 4 * q:4 * q + 4], fwd[:, q, :], e_ap, start=True, stop=True)
                    last.then_inc(s["ah_done"], 1)
                    pe.wait_ge(s["rinv_ready"], l + 1)
                    masks()
                    pe.wait_ge(s["qd_ready"], l + 1)
                    pe.wait_ge(s["qp_ready"], l + 1)
                    for q in range(2):
                        for h in range(2):
                            mm(bank[1 - par][h * J:(h + 1) * J, 0:P], uh[:, q, :], qv[:, q, 2 * h:2 * h + 2, :], start=False, stop=False, skip_group_check=True)

            pe.wait_ge(s["hist_done"], 2 * S)
            pe.wait_ge(s["fin_in"], 48)
            pe.wait_ge(s["w1_in"], 96)
            for c in range(NCH):
                for h in range(2):
                    mm(bank[4 + h][0:J, 0:256], hy[:, h, :], ahist[:, c * CL:(c + 1) * CL, 2 * h:2 * h + 2], start=True, stop=False)
                    mm(bank[4 + h][0:J, 0:256], lsyT[:], shist[:, c * CL:(c + 1) * CL, 2 * h:2 * h + 2], start=False, stop=True).then_inc(s["y_done"], 1)
                pe.wait_ge(s["u_ready"], 2 * c + 2)
                for b in range(B):
                    k = c * B + b
                    pe.wait_ge(s["x_added"], 2 * B + 2 * B * c + max(b - 1, 0))
                    mm(bank[6 + b % 2][:], uT[:, b, :], lyy[:], start=True, stop=True).then_inc(s["yy_done"], 1)
                for b in range(B):
                    transposes(24 + c * B + b)
                pe.wait_ge(s["xT_ready"], 24 + c * B + B)
                for b in range(B + 1):
                    k = c * B + b
                    if b < B:
                        if k >= 2:
                            pe.wait_ge(s["pe_exp"], k - 1)
                        for kt in range(KT):
                            last = mm(bank[2 + k % 2][:, 0:NE], xT[:, kt, b * CL:(b + 1) * CL], gwT[:, kt, :], start=(kt == 0), stop=(kt == KT - 1))
                        last.then_inc(s["lg_done"], 1)
                    if b >= 1:
                        k -= 1
                        pe.wait_ge(s["wsel_ready"], k + 1)
                        if k >= 2:
                            pe.wait_ge(s["wT_ready"], k - 1)
                        nc.tensor.transpose(bank[4 + k % 2][0:NE, 0:P], wsel[:, k % 2, 0, :], ident[:]).then_inc(s["wt_done"], 1)
                pe.wait_ge(s["wT_ready"], c * B + B)
                gate_up(2 * IT0 + c * IT1, IT1, w1g, w1u, True)
                down(2 * IT0 + c * IT1, IT1, w1d, 2 * B + 2 * B * c + B)


def kernel(**inputs):
    import concourse.bacc as bacc
    from concourse.bass_utils import run_bass_kernel_spmd

    i = {k: np.asarray(v) for k, v in inputs.items()}
    ctx = i["ctx_1024"]
    perm = np.concatenate([np.arange(q * J, (q + 1) * J) for q in (1, 2, 0, 3)])
    kT = ctx.reshape(B, T, 8, HD).transpose(2, 3, 0, 1)
    krep = np.repeat(kT[:, None], 4, 1).reshape(KT, P, B, T).transpose(1, 0, 2, 3)
    arrays = {
        "x": i["x"], "ctx_1024": ctx, "mask_SxS2_ff0": i["mask_SxS2_ff0"], "krep": krep,
        "lens": i["_lenS2"].reshape(1, B),
        "gate_qT": i["L0_ffn_gate_q"].T, "gate_sT": i["L0_ffn_gate_s"].T,
        "up_qT": i["L0_ffn_up_q"].T, "up_sT": i["L0_ffn_up_s"].T,
        "down_qT": i["L0_ffn_down_q"].T, "down_sT": i["L0_ffn_down_s"].T,
        "LysT": i["L1_xattn_L_ys"][perm].T, "LssT": i["L1_xattn_L_ss"][perm].T,
        "LgsT": i["L1_xattn_L_gs_w"][perm].T, "gsb2": i["L1_xattn_L_gs_b"][perm].reshape(2, P).T,
        "LgyT": i["L1_xattn_L_gy_w"].T, "LsyT": i["L1_xattn_L_sy"].T, "bgy": i["L1_xattn_L_gy_b"].reshape(J, 1),
        "LyyT": i["L1_xattn_L_yy_w"].T, "byy": i["L1_xattn_L_yy_b"].reshape(1, H),
        "ctxT": ctx.reshape(2, P, D).transpose(2, 0, 1),
        "WahT": i["L1_xattn_Wa_h"].T, "WasT": i["L1_xattn_Wa_s"].T, "WafT": i["L1_xattn_Wa_f"].T,
        "convw": i["L1_xattn_conv_w"].reshape(FCH, KW), "ba": i["L1_xattn_ba"].reshape(J, 1), "va": i["L1_xattn_va"].reshape(J, 1),
        "gwT": i["L1_ffn_gate_w"].T, "g1T": i["L1_ffn_g"].T, "u1T": i["L1_ffn_u"].T, "d1T": i["L1_ffn_d"].T,
        **shape_constants(),
    }
    arrays = {"d_" + k: np.ascontiguousarray(v) for k, v in arrays.items()}
    nc = bacc.Bacc("TRN2", target_bir_lowering=False, num_devices=1)
    aps = {k[2:]: nc.dram_tensor(k, v.shape, mybir.dt.from_np(v.dtype), kind="ExternalInput").ap() for k, v in arrays.items()}
    out = nc.dram_tensor("d_out", (B, S, H), F32, kind="ExternalOutput").ap()
    build(nc, aps, out)
    r = run_bass_kernel_spmd(nc, [arrays], core_ids=[0])
    return r.results[0]["d_out"]
```

```python
from contextlib import ExitStack

import numpy as np

import concourse.bass as bass
from concourse import mybir

ALU = mybir.AluOpType
ACT = mybir.ActivationFunctionType
F32 = mybir.dt.float32
F16 = mybir.dt.float16
BF16 = mybir.dt.bfloat16
I32 = mybir.dt.int32
U32 = mybir.dt.uint32
AX = mybir.AxisListType

P = 128
B, S, H = 4, 256, 512
T, D = 64, 128
NCH = 2
CL = S // NCH
KT = H // P
HEADS, HD = 32, 16
I0, IT0 = 1792, 14
NE, EI = 16, 56
I1, IT1 = NE * EI, NE * EI // P
J = 64
KW = 101
FCH = 10
TH = T // 2
NF = T
BIG = 1.0e30
EPS = 1e-5


def shape_constants():
    t = np.arange(TH)
    k = np.arange(KW) - KW // 2
    fwd, inv = np.zeros((P, TH)), np.zeros((P, TH))
    ker = np.zeros((3, P, KW))
    r = 0
    for m in range(NF // 2 + 1):
        w = 2 * np.pi * m / NF
        edge = m in (0, NF // 2)
        c = (1.0 if edge else 2.0) / NF
        cos, sin = np.cos, np.sin
        for fa, fb, fc, sign in ((cos, cos, cos, 1), (cos, sin, sin, -1), (sin, sin, cos, 1), (sin, cos, sin, 1)):
            fwd[r], inv[r] = fa(w * t), fb(w * t)
            for d in (-1, 0, 1):
                lag = k - TH * d
                ker[d + 1, r] = sign * c * fc(w * lag) * (np.abs(lag) < TH)
            r += 1
            if edge:
                break
    f32 = np.float32
    fwd4 = np.tile(fwd.T, (B, 1))
    fwd_hi = fwd4.astype(np.float16)
    bm = np.arange(P) // TH
    four = np.arange(B)[:, None]
    return {
        "c_ident": np.eye(P, dtype=f32),
        "c_fwd": np.stack([fwd_hi, (fwd4 - fwd_hi).astype(np.float16)], 1),
        "c_inv": inv.astype(f32),
        "c_ker": ker.transpose(2, 0, 1).astype(f32),
        "c_headsel": (np.arange(P)[:, None] // HD == np.arange(8)[None]).astype(f32),
        "c_expert": (np.arange(I1)[None] // EI == np.arange(NE)[:, None]).astype(f32),
        "c_iota": np.tile(np.arange(NE, dtype=f32), (P, 1)),
        "c_time": np.tile(np.arange(T, dtype=f32), (B, 1)),
        "c_time2": np.stack([np.tile(np.arange(TH), B), np.tile(np.arange(TH, T), B)]).astype(f32),
        "c_gatescale": np.stack([np.where(np.arange(P) < J, 1.0, 2.0), np.ones(P)], 1).astype(f32),
        "c_batchsel": (bm[None] == four).astype(f32),
        "c_half_batch": np.concatenate([np.repeat(np.eye(2), B, 1), np.tile(-2 * BIG * (np.arange(B)[None] != four), (1, 2))]).astype(f32),
    }


def build(nc, a, out):
    with ExitStack() as ctx:
        def sb(name, shape, dt=F32):
            return ctx.enter_context(nc.sbuf_tensor(name, shape, dt))

        def sem(name):
            return ctx.enter_context(nc.semaphore(name))

        x_sb = sb("x_sb", [P, NCH * B, H])
        xn = sb("xn", [P, 2, H])
        xT = sb("xT", [P, KT, B * CL])
        stats = sb("stats", [P, 2, 6])
        mv = sb("mv", [P, 2, 2])
        rstd = sb("rstd", [P, 2, 1])
        vareps = sb("vareps", [P, 1])
        minus_half = sb("minus_half", [P, 1])
        krep = sb("krep", [P, KT, B, T])
        headsel = sb("headsel", [P, 8])
        kbd = sb("kbd", [P, 2, 512])
        vbd = sb("vbd", [P, B, 8, 34])
        mask_sb = sb("mask_sb", [P, NCH, T])
        smax = sb("smax", [P, 32])
        rsum = sb("rsum", [P, HEADS])
        wbig = sb("wbig", [P, 2 * KT * I0 + IT0 * H])
        sscale = sb("sscale", [P, 2, I0])
        interT = sb("interT", [P, IT0, B * CL])
        sc = interT[:, 0:4, :]
        pT = interT[:, 4:6, :]
        tanh_sb = sb("tanh_sb", [P, 2, 512])
        act_sb = sb("act_sb", [P, 2, 512])
        otmp = act_sb[:, 0, :]
        lys = sb("lys", [P, KT, 256])
        gbias = sb("gbias", [P, 2])
        gscale = sb("gscale", [P, 2])
        rin = sb("rin", [P, S, 8])
        ident = sb("ident", [P, P])
        identb = sb("identb", [P, P], BF16)
        ctxT = sb("ctxT", [P, 2, P])
        wahT = sb("wahT", [P, J])
        ba2 = sb("ba2", [P, 1])
        lgsT = sb("lgsT", [P, 256])
        lgyT = sb("lgyT", [P, J])
        lssT = sb("lssT", [J, 256])
        lss3 = sb("lss3", [J, 3, 256], BF16)
        lsyT = sb("lsyT", [J, J])
        wasT = sb("wasT", [J, P])
        convw = sb("convw", [FCH, KW])
        wafT = sb("wafT", [FCH, J])
        va2 = sb("va2", [P, 1])
        vah = sb("vah", [P, 2, TH], BF16)
        vae = sb("vae", [P, 2, B])
        fwd = sb("fwd", [P, 2, P], F16)
        inv = sb("inv", [P, TH])
        ker = sb("ker", [KW, 3, P])
        u_sb = sb("u_sb", [KW, J])
        uh = sb("uh", [P, 2, P])
        enc = sb("enc", [P, P])
        enc3 = sb("enc3", [P, 3, P], BF16)
        hg = sb("hg", [P, 2, 256])
        hg3 = interT[:, 7:9, :].rearrange("p a n -> p (a n)").bitcast(BF16)[:, 0:1536].rearrange("p (j h g) -> p j h g", j=3, h=2)
        hy = sb("hy", [P, 2, J])
        onesb = sb("onesb", [P, P], BF16)
        lens = sb("lens", [B, 1], I32)
        lens2 = sb("lens2", [2, B], I32)
        lensf = sb("lensf", [B, 1])
        lens2f = sb("lens2f", [2, B])
        time = sb("time", [B, T])
        time2 = sb("time2", [2, P])
        bsel_f = sb("bsel_f", [B, P])
        etl_f = sb("etl_f", [2 + B, P])
        etr_f = sb("etr_f", [2 + B, 8])
        bsel = sb("bsel", [B, P], BF16)
        maskb = sb("maskb", [B, T], BF16)
        etl = sb("etl", [2 + B, P], BF16)
        etr = sb("etr", [2 + B, 8], BF16)
        bgy = sb("bgy", [J, 1])
        th = interT[:, 6, 0:P]
        nmx = sb("nmx", [P, 1])
        eh = sb("eh", [P, 8], F16)
        el = sb("el", [P, 8], F16)
        ex = sb("ex", [P, 2, 8])
        rinv = sb("rinv", [P, 2, B])
        g1 = sb("g1", [P, 8])
        gat = sb("gat", [P, 8])
        rs = sb("rs", [P, 8])
        ahn = sb("ahn", [P, 8])
        sh = sb("sh", [J, B], F16)
        sl = sb("sl", [J, B], F16)
        qv = krep[:, 0, :, :].rearrange("p b t -> p (b t)").rearrange("p (i b t) -> p i b t", i=2, b=B)
        tfi = sb("tfi", [J, 8])
        xs = sb("xs", [J, 2, 12])
        ab = sb("ab", [J, 8])
        tc_sb = sb("tc_sb", [J, B])
        s2 = sb("s2", [J, 2, B])
        gwT = sb("gwT", [P, KT, NE])
        probs = sb("probs", [P, 2, NE])
        top8 = sb("top8", [P, 2, 8])
        idx8 = sb("idx8", [P, 2, 8], U32)
        idxf = sb("idxf", [P, 2, 2])
        small = sb("small", [P, 2, 4])
        wsel = sb("wsel", [P, 2, 2, NE])
        iota = sb("iota", [P, NE])

        reuse = sscale[:].rearrange("p a b -> p (a b)")
        ahist = reuse[:, 0:S * 8].rearrange("p (l b) -> p l b", b=8)
        shist = reuse[0:J, S * 8:S * 12].rearrange("p (l b) -> p l b", b=B)
        uT = reuse[0:J + 1, S * 12:S * 12 + B * CL].rearrange("p (b l) -> p b l", b=B)

        ahist2 = ahist.rearrange("p (i two) b -> p i two b", two=2)
        shist2 = shist.rearrange("p (i two) b -> p i two b", two=2)
        rin2 = rin[:].rearrange("p (i two) b -> p i two b", two=2)

        bank = [ctx.enter_context(nc.psum_tensor(f"bank{i}", [P, 512], F32)) for i in range(8)]

        nw = KT * I0
        wg = wbig[:, 0:nw].rearrange("p (k o) -> p k o", k=KT)
        wu = wbig[:, nw:2 * nw].rearrange("p (k o) -> p k o", k=KT)
        wd = wbig[:, 2 * nw:].rearrange("p (k o) -> p k o", k=IT0)
        m1 = KT * I1
        w1g = wbig[:, 0:m1].rearrange("p (k o) -> p k o", k=KT)
        w1u = wbig[:, m1:2 * m1].rearrange("p (k o) -> p k o", k=KT)
        w1d = wbig[:, 2 * m1:2 * m1 + IT1 * H].rearrange("p (k o) -> p k o", k=IT1)

        lyy = wbig[0:J + 1, 3 * m1 + I1:3 * m1 + I1 + H]
        expert = wbig[0:NE, 3 * m1:3 * m1 + I1]

        wT = wbig[0:NE, 3 * m1 + I1 + H:3 * m1 + I1 + H + B * CL]

        names = """vareps_ready mv_ready rstd_ready x_in attn_in w0_in sc_in rec_in setup_in w1_in fin_in out_done
            gdeq_in ln_ready tr_done xT_ready chain pchain achain
            kbd_ready score_done score_read sub_done exp_done pt_done pt_copied av_done attn_done
            deq0 deq1 gu_done th_done inter_done down_done x_added
            rec_done rin_ready
            vbd_zero setup_v setup_mm setup_ps setup_cp setup_a mask_ready scale_ready
            pre_done th_s eb_done et_done mx_ready eh_ready ex_ready el_ready ah_done hg_done rinv_ready ahn_ready
            prod_ready g_ready q_ready tg_ready ab_ready c_ready tc_ready s_ready sh_ready sl_ready sp_done
            hist_done part_ready
            y_done u_ready yy_done lg_done lgx_ready pe_exp wsel_ready wt_done wT_ready""".split()
        s = {n: sem("s_" + n) for n in names}
        w_sc = [sem(f"s_scl{i}") for i in range(2)]
        w_in = [sem(f"s_w{i}") for i in range(3)]
        x_in = [sem(f"s_x{i}") for i in range(2)]

        block = ctx.enter_context(nc.Block())
        SETUP = 25
        DPART = [(0, 3), (3, 6), (6, 9), (9, 12), (12, 14)]

        @block.sync
        def _(sp):
            for c in range(NCH):
                sp.dma_start(x_sb[:, c * B:(c + 1) * B, :], a["x"][:, c * CL:(c + 1) * CL, :].rearrange("b p h -> p b h")).then_inc(x_in[c], 16)
                if c == 0:
                    sp.dma_start(ident[:], a["c_ident"]).then_inc(s["attn_in"], 16)
                    sp.dma_start(headsel[:], a["c_headsel"]).then_inc(s["attn_in"], 16)
                    sp.dma_start(krep[:], a["krep"]).then_inc(s["attn_in"], 16)
                    sp.dma_start(mask_sb[:], a["mask_SxS2_ff0"].rearrange("(c p) t -> p c t", p=P)).then_inc(s["attn_in"], 16)
                    sp.wait_ge(s["vbd_zero"], 1)
                    for b in range(B):
                        v = a["ctx_1024"][b].rearrange("t (g d) -> t g d", g=8)
                        for h in range(2):
                            sp.dma_start(vbd[h * T:(h + 1) * T, b, :, h * 17:h * 17 + HD], v).then_inc(s["attn_in"], 16)
            for i, (dst, src) in enumerate(((wg, a["gate_qT"]), (wu, a["up_qT"]), (wd, a["down_qT"]))):
                sp.dma_start(dst.bitcast(I32), src.rearrange("(k p) o -> p k o", p=P)).then_inc(w_in[i], 16)
            for n in range(8 + len(DPART)):
                if n >= 2:
                    sp.wait_ge(s["deq0"], n - 1)
                if n < 8:
                    src = a["gate_sT"] if n < 4 else a["up_sT"]
                    sp.dma_start(sscale[:, n % 2, :], src[n % 4:n % 4 + 1, :].partition_broadcast(P)).then_inc(w_sc[n % 2], 16)
                else:
                    i0, i1 = DPART[n - 8]
                    sp.dma_start(sscale[:, n % 2, 0:(i1 - i0) * H],
                                 a["down_sT"][i0:i1, :].rearrange("g h -> (g h)").unsqueeze(0).partition_broadcast(P)).then_inc(w_sc[n % 2], 16)
            sp.dma_start(lys[:], a["LysT"].rearrange("(k p) o -> p k o", p=P)).then_inc(s["rec_in"], 16)
            sp.dma_start(gbias[:], a["gsb2"]).then_inc(s["rec_in"], 16)
            sp.dma_start(gscale[:], a["c_gatescale"]).then_inc(s["rec_in"], 16)
            small_loads = [(ctxT[:], a["ctxT"]), (wahT[:], a["WahT"]), (lgsT[:], a["LgsT"]), (lgyT[:], a["LgyT"]),
                           (lssT[:], a["LssT"]), (lsyT[:], a["LsyT"]), (convw[:], a["convw"]),
                           (wafT[:], a["WafT"]), (fwd[:], a["c_fwd"]), (inv[:], a["c_inv"]), (ker[:], a["c_ker"]),
                           (lens[:], a["lens"]), (time[:], a["c_time"]), (time2[:], a["c_time2"]),
                           (bsel_f[:], a["c_batchsel"]), (etl_f[2:2 + B, :], a["c_batchsel"]), (etr_f[:], a["c_half_batch"])]
            for h in range(2):
                small_loads.append((ba2[h * J:(h + 1) * J, :], a["ba"]))
                small_loads.append((va2[h * J:(h + 1) * J, :], a["va"]))
                small_loads.append((wasT[:, h * J:(h + 1) * J], a["WasT"]))
                small_loads.append((lens2[h:h + 1, :], a["lens"].rearrange("b o -> o b")))
            assert len(small_loads) == SETUP
            for dst, src in small_loads:
                sp.dma_start(dst, src).then_inc(s["setup_in"], 16)
            for dst, src in ((bgy[:], a["bgy"]), (gwT[:], a["gwT"].rearrange("(k p) e -> p k e", p=P)), (iota[:], a["c_iota"])):
                sp.dma_start(dst, src).then_inc(s["fin_in"], 16)
            sp.wait_ge(s["down_done"], 2 * B)
            for dst, src in ((w1g, a["g1T"]), (w1u, a["u1T"]), (w1d, a["d1T"])):
                sp.dma_start(dst, src.rearrange("(k p) o -> p k o", p=P)).then_inc(s["w1_in"], 16)
            for dst, src in ((expert, a["c_expert"]), (lyy[0:J, :], a["LyyT"]), (lyy[J:J + 1, :], a["byy"])):
                sp.dma_start(dst, src).then_inc(s["w1_in"], 16)
            for k in range(NCH * B):
                c, b = divmod(k, B)
                sp.wait_ge(s["x_added"], 2 * B + 2 * B * c + B + b + 1)
                sp.dma_start(out[b, c * CL:(c + 1) * CL, :], x_sb[:, k, :]).then_inc(s["out_done"], 16)
            sp.wait_ge(s["out_done"], 16 * NCH * B)

        @block.gpsimd
        def _(pool):
            nc.gpsimd.memset(vbd[:], 0.0).then_inc(s["pchain"], 1)
            nc.gpsimd.memset(onesb[:], 1.0)
            nc.gpsimd.memset(minus_half[:], -0.5)
            pool.wait_ge(s["pchain"], 1)
            nc.gpsimd.memset(vbd[0:T, :, :, 16:17], 1.0).then_inc(s["pchain"], 1)
            pool.wait_ge(s["pchain"], 2)
            nc.gpsimd.memset(vbd[T:P, :, :, 33:34], 1.0).then_inc(s["vbd_zero"], 1)
            def rstd_of(n):
                pool.wait_ge(s["mv_ready"], n + 1)
                nc.gpsimd.tensor_scalar(vareps[:], mv[:, n % 2, 1:2], EPS, None, ALU.add).then_inc(s["vareps_ready"], 1)
                pool.wait_ge(s["vareps_ready"], n + 1)
                nc.gpsimd.tensor_tensor(rstd[:, n % 2, :], vareps[:], minus_half[:], ALU.pow).then_inc(s["rstd_ready"], 1)

            pool.wait_ge(s["attn_in"], 16 * 12)
            for k in range(NCH * B):
                b = k % B
                rstd_of(12 * (k // B) + b)
                for kt in range(KT):
                    n = k * KT + kt
                    if n >= 2:
                        pool.wait_ge(s["score_done"], n - 1)
                    nc.gpsimd.tensor_tensor(
                        kbd[:, n % 2, :].rearrange("p (h t) -> p h t", h=8),
                        krep[:, kt, b, :].unsqueeze(1).broadcast_to([P, 8, T]),
                        headsel[:].unsqueeze(2).broadcast_to([P, 8, T]), ALU.mult).then_inc(s["kbd_ready"], 1)
                if b == B - 1:
                    for j in range(B, 3 * B):
                        rstd_of(12 * (k // B) + j)
            pool.wait_ge(s["setup_in"], 16 * SETUP)
            nc.gpsimd.tensor_scalar(lssT[:, 0:J], lssT[:, 0:J], 0.5, None, ALU.mult)
            nc.gpsimd.tensor_scalar(lssT[:, 2 * J:4 * J], lssT[:, 2 * J:4 * J], 0.5, None, ALU.mult)
            nc.gpsimd.tensor_scalar(lsyT[:], lsyT[:], 0.5, None, ALU.mult)
            nc.gpsimd.tensor_scalar(wasT[:], wasT[:], 0.5, None, ALU.mult)
            nc.gpsimd.tensor_scalar(lgsT[:, J:2 * J], lgsT[:, J:2 * J], 2.0, None, ALU.mult).then_inc(s["scale_ready"], 1)
            nc.gpsimd.memset(xs[:], 0.0)
            nc.gpsimd.memset(s2[:], 0.0).then_inc(s["s_ready"], 1)
            nc.gpsimd.memset(sh[:], 0.0)
            nc.gpsimd.memset(sl[:], 0.0).then_inc(s["sl_ready"], 1)
            nc.gpsimd.memset(vah[:], 0.0)
            nc.gpsimd.memset(vae[:], 0.0).then_inc(s["pchain"], 1)
            pool.wait_ge(s["deq0"], 8 + len(DPART))
            pool.wait_ge(s["pchain"], 3)
            nc.gpsimd.memset(uT[J:J + 1, :, :], 1.0).then_inc(s["pchain"], 1)
            pool.wait_ge(s["pchain"], 4)
            nc.gpsimd.tensor_copy(vah[0:J, 0, :], va2[0:J, 0:1].broadcast_to([J, TH]))
            nc.gpsimd.tensor_copy(vae[0:J, 0, :], va2[0:J, 0:1].broadcast_to([J, B])).then_inc(s["pchain"], 1)
            pool.wait_ge(s["pchain"], 5)
            nc.gpsimd.tensor_copy(vah[J:P, 1, :], va2[J:P, 0:1].broadcast_to([J, TH]))
            nc.gpsimd.tensor_copy(vae[J:P, 1, :], va2[J:P, 0:1].broadcast_to([J, B])).then_inc(s["setup_v"], 1)
            pool.wait_ge(s["setup_v"], 1)
            nc.gpsimd.tensor_copy(identb[:], ident[:]).then_inc(s["hist_done"], 4)

            with pool.Fori(0, S // 2) as i:
                for par in range(2):
                    l = i * 2 + par
                    pool.wait_ge(s["s_ready"], l + 1)
                    nc.gpsimd.tensor_copy(shist2[:, bass.ds(i, 1), par, :], s2[:, par:par + 1, :]).then_inc(s["hist_done"], 1)
                    pool.wait_ge(s["rinv_ready"], l + 1)
                    nc.gpsimd.tensor_tensor(ahist2[:, bass.ds(i, 1), par, :].rearrange("p one (o b) -> p (one o) b", o=2),
                                            ex[:, par, :].rearrange("p (o b) -> p o b", o=2),
                                            rinv[:, par:par + 1, :].broadcast_to([P, 2, B]), ALU.mult).then_inc(s["hist_done"], 1)

            for n in range(6 * B, 8 * B):
                rstd_of(n)

        @block.vector
        def _(dve):
            chain = [0]

            def link(ins):
                chain[0] += 1
                ins.then_inc(s["chain"], 1)
                dve.wait_ge(s["chain"], chain[0])

            def layernorm(n, k):
                if n >= 2:
                    dve.wait_ge(s["tr_done"], n - 1)
                q = n % 2
                link(nc.vector.bn_stats(stats[:, q, :], x_sb[:, k, :]))
                nc.vector.bn_aggr(mv[:, q, :], stats[:, q, :]).then_inc(s["mv_ready"], 1)
                dve.wait_ge(s["rstd_ready"], n + 1)
                nc.vector.tensor_scalar(xn[:, q, :], x_sb[:, k, :], mv[:, q, 0:1], rstd[:, q, 0:1],
                                        ALU.subtract, ALU.mult).then_inc(s["ln_ready"], 1)

            def attention(k):
                c = k // B
                for kt in range(KT):
                    n = k * KT + kt
                    dve.wait_ge(s["score_done"], n + 1)
                    if kt == 0 and k > 0:
                        dve.wait_ge(s["pt_done"], 4 * k)
                    v = sc[:, kt, :].rearrange("p (h t) -> p h t", h=8)
                    link(nc.vector.scalar_tensor_tensor(
                        v, bank[2 + n % 2][:].rearrange("p (h t) -> p h t", h=8), 0.25,
                        mask_sb[:, c:c + 1, :].broadcast_to([P, 8, T]), ALU.mult, ALU.add))
                    sc_max = smax[:, kt * 8:(kt + 1) * 8]
                    ins = nc.vector.tensor_reduce(sc_max, v, AX.X, ALU.max)
                    link(ins)
                    nc.vector.tensor_tensor(v, v, sc_max.unsqueeze(2).broadcast_to([P, 8, T]), ALU.subtract).then_inc(s["sub_done"], 1)
                dve.wait_ge(s["av_done"], k + 1)
                for h in range(2):
                    o = bank[6 + h][:, 0:272].rearrange("p (h e) -> p h e", e=17)
                    r = rsum[:, 16 * h:16 * h + 16]
                    link(nc.vector.reciprocal(r.unsqueeze(2), o[:, :, 16:17]))
                    link(nc.vector.tensor_tensor(otmp[:, 256 * h:256 * h + 256].rearrange("p (h d) -> p h d", d=HD), o[:, :, 0:HD],
                                                 r.unsqueeze(2).broadcast_to([P, 16, HD]), ALU.mult))
                ins = nc.vector.tensor_tensor(x_sb[:, k, :], x_sb[:, k, :], otmp, ALU.add)
                chain[0] += 1
                ins.then_inc(s["chain"], 1)
                dve.wait_ge(s["chain"], chain[0])

            def dequantise():
                for n in range(8 + len(DPART)):
                    dve.wait_ge(w_in[min(n // 4, 2)], 16)
                    dve.wait_ge(w_sc[n % 2], 16 * (n // 2 + 1))
                    if n < 8:
                        w = (wg if n < 4 else wu)[:, n % 4, :]
                        sc_ap = sscale[:, n % 2, :]
                    else:
                        i0, i1 = DPART[n - 8]
                        w = wd[:, i0:i1, :].rearrange("p k o -> p (k o)")
                        sc_ap = sscale[:, n % 2, 0:(i1 - i0) * H]
                    nc.vector.tensor_tensor(w, w.bitcast(I32), sc_ap, ALU.mult).then_inc(s["deq0"], 1)

            def swiglu(base, tiles, expert_weights):
                for it in range(tiles):
                    n = base + it
                    dve.wait_ge(s["th_done"], n + 1)
                    if n >= 2:
                        pass
                    q = n % 2
                    link(nc.vector.scalar_tensor_tensor(act_sb[:, q, :], tanh_sb[:, q, :], 1.0, bank[2 + q][:], ALU.add, ALU.mult))
                    if expert_weights:
                        link(nc.vector.scalar_tensor_tensor(act_sb[:, q, :], act_sb[:, q, :], 0.5, bank[4 + q][:], ALU.mult, ALU.mult))
                        nc.vector.tensor_tensor(interT[:, it, :], act_sb[:, q, :], bank[q][:], ALU.mult).then_inc(s["inter_done"], 1)
                    else:
                        nc.vector.scalar_tensor_tensor(interT[:, it, :], act_sb[:, q, :], 0.5, bank[4 + q][:], ALU.mult, ALU.mult).then_inc(s["inter_done"], 1)

            added = [0]

            def add_residual(k, bk, ready, count):
                dve.wait_ge(ready, count)
                added[0] += 1
                nc.vector.tensor_tensor(x_sb[:, k, :], x_sb[:, k, :], bk[:], ALU.add).then_inc(s["x_added"], 1)
                dve.wait_ge(s["x_added"], added[0])

            for c in range(NCH):
                dve.wait_ge(x_in[c], 16)
                for b in range(B):
                    layernorm(12 * c + b, c * B + b)
                    attention(c * B + b)
                if c == 0:
                    dequantise()
                for b in range(B):
                    layernorm(12 * c + 4 + b, c * B + b)
                swiglu(c * IT0, IT0, False)
                for b in range(B):
                    add_residual(c * B + b, bank[6 + b % 2], s["down_done"], c * B + b + 1)
                    layernorm(12 * c + 8 + b, c * B + b)

            dve.wait_ge(s["setup_in"], 16 * SETUP)
            nc.vector.tensor_copy(lensf[:], lens[:])
            link(nc.vector.tensor_copy(lens2f[:], lens2[:]))
            nc.vector.tensor_scalar(maskb[:], time[:], lensf[:, 0:1], -BIG, ALU.is_ge, ALU.mult)
            link(nc.vector.tensor_tensor(time2[:].rearrange("p (b t) -> p b t", b=B), time2[:].rearrange("p (b t) -> p b t", b=B),
                                         lens2f[:].unsqueeze(2).broadcast_to([2, B, TH]), ALU.is_ge))
            link(nc.vector.tensor_scalar(etl_f[0:2, :], time2[:], -BIG, None, ALU.mult))
            nc.vector.tensor_copy(etl[:], etl_f[:])
            nc.vector.tensor_copy(etr[:], etr_f[:])
            nc.vector.tensor_copy(bsel[:], bsel_f[:]).then_inc(s["mask_ready"], 1)

            def in_parts(dst, src):
                for j in range(3):
                    link(nc.vector.tensor_copy(dst[:, j], src))
                    if j < 2:
                        link(nc.vector.tensor_tensor(src, src, dst[:, j], ALU.subtract))

            dve.wait_ge(s["scale_ready"], 1)
            in_parts(lss3[:], lssT[:])
            dve.wait_ge(s["setup_cp"], 2)
            in_parts(enc3[:], enc[:])
            in_parts(hg3, hg[:])
            nc.vector.tensor_copy(mv[0:1, 0, 0:1], mv[0:1, 0, 1:2]).then_inc(s["part_ready"], 1)

            def by_half(ap):
                return ap.rearrange("p (o b) -> p o b", o=2)

            with dve.Fori(0, S // 2) as i:
                for par in range(2):
                    l = i * 2 + par
                    norm = rinv[:, par:par + 1, :].broadcast_to([P, 2, B])
                    dve.wait_ge(s["sp_done"], l + 1)
                    nc.vector.tensor_tensor(rs[:].unsqueeze(1), bank[6][:, 0:8].unsqueeze(1), rin2[:, bass.ds(i, 1), par, :], ALU.add)
                    dve.wait_ge(s["eb_done"], l + 1)
                    nc.vector.tensor_reduce(nmx[:], bank[2][:, 0:T], AX.X, ALU.max, negate=True).then_inc(s["mx_ready"], 1)
                    dve.wait_ge(s["ex_ready"], l + 1)
                    nc.vector.tensor_tensor(el[:], ex[:, par, :], eh[:], ALU.subtract).then_inc(s["el_ready"], 1)
                    dve.wait_ge(s["ah_done"], l + 1)
                    nc.vector.reciprocal(rinv[:, par, :], bank[5][:, 8:12]).then_inc(s["rinv_ready"], 1)
                    dve.wait_ge(s["rinv_ready"], l + 1)
                    nc.vector.tensor_tensor(by_half(ahn[:]), by_half(bank[5][:, 0:8]), norm, ALU.mult).then_inc(s["ahn_ready"], 1)
                    dve.wait_ge(s["hg_done"], l + 1)
                    nc.vector.tensor_tensor(by_half(g1[:]), by_half(bank[4][:, 0:8]), norm, ALU.mult).then_inc(s["prod_ready"], 1)
                    dve.wait_ge(s["prod_ready"], l + 1)
                    nc.vector.tensor_tensor(gat[:], g1[:], rs[:], ALU.add).then_inc(s["g_ready"], 1)
                    dve.wait_ge(s["ahn_ready"], l + 1)
                    nc.vector.tensor_tensor(qv.rearrange("p i b t -> p (i b) t"), inv[:].unsqueeze(1).broadcast_to([P, 8, TH]),
                                            ahn[:].unsqueeze(2).broadcast_to([P, 8, TH]), ALU.mult).then_inc(s["q_ready"], 1)
                    dve.wait_ge(s["tg_ready"], l + 1)
                    nc.vector.scalar_tensor_tensor(ab[:], tfi[:], 1.0, xs[:, par, 0:8], ALU.add, ALU.mult).then_inc(s["ab_ready"], 1)
                    dve.wait_ge(s["ab_ready"], l + 1)
                    nc.vector.scalar_tensor_tensor(xs[:, 1 - par, 0:4], ab[:, 0:4], 0.5, ab[:, 4:8], ALU.mult, ALU.add).then_inc(s["c_ready"], 1)
                    dve.wait_ge(s["hist_done"], 2 * l + 4)
                    dve.wait_ge(s["tc_ready"], l + 1)
                    nc.vector.scalar_tensor_tensor(s2[:, 1 - par, :], xs[:, par, 8:12], 1.0, tc_sb[:], ALU.add, ALU.mult).then_inc(s["s_ready"], 1)
                    dve.wait_ge(s["s_ready"], l + 2)
                    nc.vector.tensor_copy(sh[:], s2[:, 1 - par, :]).then_inc(s["sh_ready"], 1)
                    dve.wait_ge(s["sh_ready"], l + 1)
                    nc.vector.tensor_tensor(sl[:], s2[:, 1 - par, :], sh[:], ALU.subtract).then_inc(s["sl_ready"], 1)

            for c in range(NCH):
                for b in range(B):
                    k = c * B + b
                    add_residual(k, bank[6 + b % 2], s["yy_done"], k + 1)
                    layernorm(24 + k, k)
                for b in range(B):
                    k = c * B + b
                    q = k % 2
                    dve.wait_ge(s["lg_done"], k + 1)
                    link(nc.vector.tensor_reduce(small[:, q, 0:1], bank[2 + q][:, 0:NE], AX.X, ALU.max, negate=True))
                    nc.vector.tensor_copy(small[:, q, 1:2], small[:, q, 0:1]).then_inc(s["lgx_ready"], 1)
                    dve.wait_ge(s["pe_exp"], k + 1)
                    link(nc.vector.max(top8[:, q, :], probs[:, q, :]))
                    nc.vector.tensor_scalar(small[:, q, 2:3], top8[:, q, 0:1], top8[:, q, 1:2], None, ALU.add)
                    link(nc.vector.max_index(idx8[:, q, :], top8[:, q, :], probs[:, q, :]))
                    link(nc.vector.reciprocal(small[:, q, 3:4], small[:, q, 2:3]))
                    link(nc.vector.tensor_copy(idxf[:, q, :], idx8[:, q, 0:2]))
                    link(nc.vector.tensor_scalar(top8[:, q, 0:2], top8[:, q, 0:2], small[:, q, 3:4], None, ALU.mult))
                    for j in range(2):
                        ins = nc.vector.tensor_scalar(wsel[:, q, j, :], iota[:], idxf[:, q, j:j + 1], top8[:, q, j:j + 1], ALU.is_equal, ALU.mult)
                    link(ins)
                    if k >= 2:
                        dve.wait_ge(s["wt_done"], k - 1)
                    link(nc.vector.tensor_tensor(wsel[:, q, 0, :], wsel[:, q, 0, :], wsel[:, q, 1, :], ALU.add))
                    nc.vector.tensor_copy(small[:, q, 2:3], small[:, q, 3:4]).then_inc(s["wsel_ready"], 1)
                swiglu(2 * IT0 + c * IT1, IT1, True)
                for b in range(B):
                    k = c * B + b
                    add_residual(k, bank[6 + b % 2], s["down_done"], 2 * B + k + 1)

        @block.scalar
        def _(act):
            def copy_xT(n, b):
                act.wait_ge(s["tr_done"], n + 1)
                nc.scalar.activation(xT[:, :, b * CL:(b + 1) * CL], bank[n % 2][:].rearrange("p (k t) -> p k t", k=KT), ACT.Copy).then_inc(s["xT_ready"], 1)

            def attention(k):
                for kt in range(KT):
                    act.wait_ge(s["sub_done"], k * KT + kt + 1)
                    nc.scalar.activation(sc[:, kt, :], sc[:, kt, :], ACT.Exp).then_inc(s["exp_done"], 1)
                for g in range(4):
                    n = 4 * k + g
                    act.wait_ge(s["pt_done"], n + 1)
                    nc.scalar.activation(pT[:, n % 2, :], bank[4 + n % 2][:], ACT.Copy).then_inc(s["pt_copied"], 1)

            def tanh_gate(base, tiles):
                for it in range(tiles):
                    n = base + it
                    act.wait_ge(s["gu_done"], n + 1)
                    if n >= 2:
                        act.wait_ge(s["inter_done"], n - 1)
                    nc.scalar.activation(tanh_sb[:, n % 2, :], bank[2 + n % 2][:], ACT.Tanh, scale=0.5).then_inc(s["th_done"], 1)

            for c in range(NCH):
                for b in range(B):
                    copy_xT(12 * c + b, b)
                    attention(c * B + b)
                for b in range(B):
                    if b == 0:
                        act.wait_ge(s["score_done"], 16 * (c + 1))
                    copy_xT(12 * c + 4 + b, b)
                tanh_gate(c * IT0, IT0)
                for b in range(B):
                    copy_xT(12 * c + 8 + b, b)
                if c == 0:
                    act.wait_ge(s["rec_in"], 48)
                    for gp in range(2):
                        last = nc.scalar.activation(gbias[:, gp:gp + 1], gbias[:, gp:gp + 1], ACT.Copy, scale=gscale[:, gp:gp + 1])
                    last.then_inc(s["achain"], 1)
                    act.wait_ge(s["achain"], 1)
                for gp in range(2):
                    act.wait_ge(s["rec_done"], 2 * c + gp + 1)
                    nc.scalar.activation(rin[:, c * CL:(c + 1) * CL, gp * 4:gp * 4 + 4].rearrange("p l b -> p b l"),
                                         bank[4 + gp][:].rearrange("p (b l) -> p b l", b=B), ACT.Identity,
                                         bias=gbias[:, gp:gp + 1], scale=gscale[:, gp:gp + 1]).then_inc(s["rin_ready"], 1)

            act.wait_ge(s["setup_mm"], 1)
            act.wait_ge(s["setup_in"], 16 * SETUP)
            nc.scalar.activation(u_sb[:], bank[0][0:KW, 0:J], ACT.Copy).then_inc(s["setup_cp"], 1)
            act.wait_ge(s["setup_mm"], 2)
            nc.scalar.activation(enc[:], bank[1][:, 0:P], ACT.Identity, bias=ba2[:, 0:1])
            nc.scalar.activation(hg[:], bank[2][:].rearrange("p (h g) -> p h g", h=2), ACT.Copy)
            nc.scalar.activation(hy[:], bank[3][:, 0:P].rearrange("p (h g) -> p h g", h=2), ACT.Copy)
            nc.scalar.activation(uh[:], bank[4][:, 0:256].rearrange("p (h g) -> p h g", h=2), ACT.Copy).then_inc(s["setup_cp"], 1)

            with act.Fori(0, S // 2) as i:
                for par in range(2):
                    l = i * 2 + par
                    act.wait_ge(s["pre_done"], l + 1)
                    nc.scalar.activation(th, bank[par][:, 0:P], ACT.Tanh).then_inc(s["th_s"], 1)
                    act.wait_ge(s["et_done"], l + 1)
                    act.wait_ge(s["mx_ready"], l + 1)
                    nc.scalar.activation(eh[:], bank[3][:, 0:8], ACT.Exp, bias=nmx[:, 0:1]).then_inc(s["eh_ready"], 1)
                    nc.scalar.activation(ex[:, par, :], bank[3][:, 0:8], ACT.Exp, bias=nmx[:, 0:1]).then_inc(s["ex_ready"], 1)
                    act.wait_ge(s["g_ready"], l + 1)
                    nc.scalar.activation(xs[:, par, 4:12], gat[J:P, :], ACT.Tanh, scale=0.5)
                    nc.scalar.activation(tfi[:], gat[0:J, :], ACT.Tanh, scale=0.5).then_inc(s["tg_ready"], 1)
                    act.wait_ge(s["c_ready"], l + 1)
                    nc.scalar.activation(tc_sb[:], xs[:, 1 - par, 0:4], ACT.Tanh, scale=0.5).then_inc(s["tc_ready"], 1)

            act.wait_ge(s["fin_in"], 48)
            for c in range(NCH):
                act.wait_ge(s["y_done"], c + 1)
                if c > 0:
                    act.wait_ge(s["yy_done"], B * c)
                nc.scalar.activation(uT[0:J, :, :], bank[4][0:J, :].rearrange("p (l b) -> p b l", b=B),
                                     ACT.Tanh, bias=bgy[:, 0:1]).then_inc(s["u_ready"], 1)
                for b in range(B):
                    if c > 0 and b == 0:
                        act.wait_ge(s["gu_done"], 2 * IT0 + c * IT1)
                    copy_xT(24 + B * c + b, b)
                for b in range(B):
                    k = c * B + b
                    q = k % 2
                    act.wait_ge(s["lgx_ready"], k + 1)
                    nc.scalar.activation(probs[:, q, :], bank[2 + q][:, 0:NE], ACT.Exp, bias=small[:, q, 1:2]).then_inc(s["pe_exp"], 1)
                    act.wait_ge(s["wt_done"], k + 1)
                    nc.scalar.activation(wT[:, b * CL:(b + 1) * CL], bank[4 + q][0:NE, 0:CL], ACT.Copy).then_inc(s["wT_ready"], 1)
                tanh_gate(2 * IT0 + c * IT1, IT1)

        @block.tensor
        def _(pe):
            mm = nc.tensor.matmul

            def transposes(n):
                pe.wait_ge(s["ln_ready"], n + 1)
                if n >= 2:
                    pe.wait_ge(s["xT_ready"], n - 1)
                for kt in range(KT):
                    last = nc.tensor.transpose(bank[n % 2][:, kt * P:(kt + 1) * P], xn[:, n % 2, kt * P:(kt + 1) * P], ident[:])
                last.then_inc(s["tr_done"], 1)

            def attention(k, n_ln):
                b = k % B
                pe.wait_ge(s["xT_ready"], n_ln + 1)
                for kt in range(KT):
                    n = k * KT + kt
                    pe.wait_ge(s["kbd_ready"], n + 1)
                    if n >= 2:
                        pe.wait_ge(s["sub_done"], n - 1)
                    mm(bank[2 + n % 2][:], xT[:, kt, b * CL:(b + 1) * CL], kbd[:, n % 2, :], start=True, stop=True).then_inc(s["score_done"], 1)
                for g in range(5):
                    if g < 4:
                        n = 4 * k + g
                        pe.wait_ge(s["exp_done"], n + 1)
                        if n >= 2:
                            pe.wait_ge(s["pt_copied"], n - 1)
                        for j in range(4):
                            last = nc.tensor.transpose(bank[4 + n % 2][:, j * P:(j + 1) * P], sc[:, g, j * P:(j + 1) * P], ident[:])
                        last.then_inc(s["pt_done"], 1)
                    if g >= 1:
                        n = 4 * k + g - 1
                        pe.wait_ge(s["pt_copied"], n + 1)
                        for j in range(4):
                            p = 4 * (g - 1) + j
                            last = mm(bank[6 + p // 8][:, (p % 8) * 34:(p % 8) * 34 + 34], pT[:, n % 2, j * P:(j + 1) * P],
                                      vbd[:, b, p // 2, :], start=True, stop=True)
                last.then_inc(s["av_done"], 1)

            def gate_up(base, tiles, g, u, weights):
                for it in range(tiles):
                    n = base + it
                    if n >= 2:
                        pe.wait_ge(s["inter_done"], n - 1)
                    if weights:
                        mm(bank[n % 2][:], expert[:, it * P:(it + 1) * P], wT[:], start=True, stop=True)
                    for w, bk in ((g, bank[2 + n % 2]), (u, bank[4 + n % 2])):
                        for kt in range(KT):
                            last = mm(bk[:], w[:, kt, it * P:(it + 1) * P], xT[:, kt, :], start=(kt == 0), stop=(kt == KT - 1))
                    last.then_inc(s["gu_done"], 1)

            added = [0]

            def down(base_inter, tiles, w, base_add):
                for b in range(B):
                    if b == 0:
                        pe.wait_ge(s["inter_done"], base_inter + tiles)
                    if b >= 2:
                        pe.wait_ge(s["x_added"], base_add + b - 1)
                    for it in range(tiles):
                        last = mm(bank[6 + b % 2][:], interT[:, it, b * CL:(b + 1) * CL], w[:, it, :], start=(it == 0), stop=(it == tiles - 1))
                    last.then_inc(s["down_done"], 1)

            pe.wait_ge(s["attn_in"], 16 * 12)
            for c in range(NCH):
                for b in range(B):
                    k = c * B + b
                    transposes(12 * c + b)
                    attention(k, 12 * c + b)
                for b in range(B):
                    transposes(12 * c + 4 + b)
                if c == 0:
                    pe.wait_ge(s["deq0"], 8 + len(DPART))
                pe.wait_ge(s["xT_ready"], 12 * c + 8)
                gate_up(c * IT0, IT0, wg, wu, False)
                down(c * IT0 + 0, IT0, wd, c * B)
                for b in range(B):
                    transposes(12 * c + 8 + b)
                pe.wait_ge(s["xT_ready"], 12 * c + 12)
                if c == 0:
                    pe.wait_ge(s["rec_in"], 48)
                for gp in range(2):
                    for kt in range(KT):
                        last = mm(bank[4 + gp][:], lys[:, kt, gp * P:(gp + 1) * P], xT[:, kt, :], start=(kt == 0), stop=(kt == KT - 1))
                    last.then_inc(s["rec_done"], 1)

            pe.wait_ge(s["setup_in"], 16 * SETUP)
            pe.wait_ge(s["scale_ready"], 1)
            pe.wait_ge(s["setup_v"], 1)
            pe.wait_ge(s["mask_ready"], 1)
            pe.wait_ge(s["rin_ready"], 4)
            mm(bank[0][0:KW, 0:J], convw[:], wafT[:], start=True, stop=True).then_inc(s["setup_mm"], 1)
            for h in range(2):
                mm(bank[1][h * J:(h + 1) * J, 0:P], wahT[:], ctxT[:, h, :], start=True, stop=True)
                mm(bank[2][:, h * 256:(h + 1) * 256], ctxT[:, h, :], lgsT[:], start=True, stop=True)
                mm(bank[3][:, h * J:(h + 1) * J], ctxT[:, h, :], lgyT[:], start=True, stop=True)
            pe.wait_ge(s["setup_cp"], 1)
            for hi in range(2):
                for ho in range(2):
                    last = mm(bank[4][:, hi * P + ho * J:hi * P + ho * J + J], ker[:, hi - ho + 1, :], u_sb[:], start=True, stop=True)
            last.then_inc(s["setup_mm"], 1)
            pe.wait_ge(s["part_ready"], 1)
            pe.wait_ge(s["hist_done"], 4)

            def masks():
                mm(bank[2][:, 0:T], bsel[:], maskb[:], start=True, stop=False, skip_group_check=True)
                mm(bank[3][:, 0:8], etl[:], etr[:], start=True, stop=False, skip_group_check=True)

            def context_part(par):
                for j in range(3):
                    mm(bank[par][:, 0:P], identb[:], enc3[:, j, :], start=(j == 0), stop=False, skip_group_check=True)

            masks()
            context_part(0)

            with pe.Fori(0, S // 2) as i:
                for par in range(2):
                    l = i * 2 + par
                    pe.wait_ge(s["s_ready"], l + 1)
                    mm(bank[par][:, 0:P], wasT[:], s2[:, par, :].unsqueeze(2).broadcast_to([J, B, TH]),
                       start=False, stop=True, skip_group_check=True).then_inc(s["pre_done"], 1)
                    pe.wait_ge(s["sl_ready"], l + 1)
                    for gp in range(2):
                        for j, st in ((0, sh), (1, sh), (2, sh), (0, sl), (1, sl)):
                            last = mm(bank[6][:, 4 * gp:4 * gp + 4], lss3[:, j, gp * P:(gp + 1) * P], st[:],
                                      start=(j == 0 and st is sh), stop=(j == 1 and st is sl))
                    last.then_inc(s["sp_done"], 1)
                    context_part(1 - par)
                    pe.wait_ge(s["th_s"], l + 1)
                    thb = th.bitcast(BF16).rearrange("p (n two) -> p n two", two=2)
                    for b in range(B):
                        for h in range(2):
                            last = mm(bank[2][b * TH:(b + 1) * TH, h * TH:(h + 1) * TH], vah[:, h, :], thb[:, b * TH:(b + 1) * TH, 1],
                                      start=False, stop=True, skip_group_check=True)
                    last.then_inc(s["eb_done"], 1)
                    mm(bank[3][:, 0:8], th, vae[:], start=False, stop=True, skip_group_check=True).then_inc(s["et_done"], 1)
                    pe.wait_ge(s["eh_ready"], l + 1)

                    def gates(parts, e, first, final):
                        for gp in range(2):
                            for j in parts:
                                for h in range(2):
                                    ins = mm(bank[4][:, 4 * gp:4 * gp + 4], hg3[:, j, h, gp * P:(gp + 1) * P], e[:, 4 * h:4 * h + 4],
                                             start=(first and gp == 0 and j == 0 and h == 0), stop=final, skip_group_check=True)
                        return ins

                    gates((0, 1, 2), eh, True, False)
                    for j in range(2):
                        mm(bank[5][:, 0:8], fwd[:, j, :], eh[:], start=(j == 0), stop=False, skip_group_check=True)
                    for h in range(2):
                        mm(bank[5][:, 8:12], onesb[:], eh[:, 4 * h:4 * h + 4], start=False, stop=False, skip_group_check=True)
                    pe.wait_ge(s["el_ready"], l + 1)
                    mm(bank[5][:, 0:8], fwd[:, 0, :], el[:], start=False, stop=True, skip_group_check=True)
                    for h in range(2):
                        last = mm(bank[5][:, 8:12], onesb[:], el[:, 4 * h:4 * h + 4], start=False, stop=True, skip_group_check=True)
                    last.then_inc(s["ah_done"], 1)
                    gates((0, 1), el, False, True).then_inc(s["hg_done"], 1)
                    masks()
                    pe.wait_ge(s["q_ready"], l + 1)
                    for h in range(2):
                        mm(bank[1 - par][:, 0:P], uh[:, h, :], qv[:, h, :, :], start=False, stop=False, skip_group_check=True)

            pe.wait_ge(s["hist_done"], 2 * S + 4)
            pe.wait_ge(s["fin_in"], 48)
            pe.wait_ge(s["w1_in"], 96)
            for c in range(NCH):
                for h in range(2):
                    mm(bank[4][0:J, :], hy[:, h, :], ahist[:, c * CL:(c + 1) * CL, 4 * h:4 * h + 4], start=(h == 0), stop=False)
                mm(bank[4][0:J, :], lsyT[:], shist[:, c * CL:(c + 1) * CL, :], start=False, stop=True).then_inc(s["y_done"], 1)
                pe.wait_ge(s["u_ready"], c + 1)
                for b in range(B):
                    k = c * B + b
                    pe.wait_ge(s["x_added"], 2 * B + 2 * B * c + max(b - 1, 0))
                    mm(bank[6 + b % 2][:], uT[:, b, :], lyy[:], start=True, stop=True).then_inc(s["yy_done"], 1)
                for b in range(B):
                    transposes(24 + c * B + b)
                pe.wait_ge(s["xT_ready"], 24 + c * B + B)
                for b in range(B + 1):
                    k = c * B + b
                    if b < B:
                        if k >= 2:
                            pe.wait_ge(s["pe_exp"], k - 1)
                        for kt in range(KT):
                            last = mm(bank[2 + k % 2][:, 0:NE], xT[:, kt, b * CL:(b + 1) * CL], gwT[:, kt, :], start=(kt == 0), stop=(kt == KT - 1))
                        last.then_inc(s["lg_done"], 1)
                    if b >= 1:
                        k -= 1
                        pe.wait_ge(s["wsel_ready"], k + 1)
                        if k >= 2:
                            pe.wait_ge(s["wT_ready"], k - 1)
                        nc.tensor.transpose(bank[4 + k % 2][0:NE, 0:P], wsel[:, k % 2, 0, :], ident[:]).then_inc(s["wt_done"], 1)
                pe.wait_ge(s["wT_ready"], c * B + B)
                gate_up(2 * IT0 + c * IT1, IT1, w1g, w1u, True)
                down(2 * IT0 + c * IT1, IT1, w1d, 2 * B + 2 * B * c + B)


def kernel(**inputs):
    import concourse.bacc as bacc
    from concourse.bass_utils import run_bass_kernel_spmd

    i = {k: np.asarray(v) for k, v in inputs.items()}
    ctx = i["ctx_1024"]
    perm = np.concatenate([np.arange(q * J, (q + 1) * J) for q in (1, 2, 0, 3)])
    kT = ctx.reshape(B, T, 8, HD).transpose(2, 3, 0, 1)
    krep = np.repeat(kT[:, None], 4, 1).reshape(KT, P, B, T).transpose(1, 0, 2, 3)
    arrays = {
        "x": i["x"], "ctx_1024": ctx, "mask_SxS2_ff0": i["mask_SxS2_ff0"], "krep": krep,
        "lens": i["_lenS2"].reshape(B, 1),
        "gate_qT": i["L0_ffn_gate_q"].T, "gate_sT": i["L0_ffn_gate_s"].T,
        "up_qT": i["L0_ffn_up_q"].T, "up_sT": i["L0_ffn_up_s"].T,
        "down_qT": i["L0_ffn_down_q"].T, "down_sT": i["L0_ffn_down_s"].T,
        "LysT": i["L1_xattn_L_ys"][perm].T, "LssT": i["L1_xattn_L_ss"][perm].T,
        "LgsT": i["L1_xattn_L_gs_w"][perm].T, "gsb2": i["L1_xattn_L_gs_b"][perm].reshape(2, P).T,
        "LgyT": i["L1_xattn_L_gy_w"].T, "LsyT": i["L1_xattn_L_sy"].T, "bgy": i["L1_xattn_L_gy_b"].reshape(J, 1),
        "LyyT": i["L1_xattn_L_yy_w"].T, "byy": i["L1_xattn_L_yy_b"].reshape(1, H),
        "ctxT": ctx.reshape(B, 2, TH, D).transpose(3, 1, 0, 2).reshape(D, 2, P),
        "WahT": i["L1_xattn_Wa_h"].T, "WasT": i["L1_xattn_Wa_s"].T, "WafT": i["L1_xattn_Wa_f"].T,
        "convw": i["L1_xattn_conv_w"].reshape(FCH, KW), "ba": i["L1_xattn_ba"].reshape(J, 1), "va": i["L1_xattn_va"].reshape(J, 1),
        "gwT": i["L1_ffn_gate_w"].T, "g1T": i["L1_ffn_g"].T, "u1T": i["L1_ffn_u"].T, "d1T": i["L1_ffn_d"].T,
        **shape_constants(),
    }
    arrays = {"d_" + k: np.ascontiguousarray(v) for k, v in arrays.items()}
    nc = bacc.Bacc("TRN2", target_bir_lowering=False, num_devices=1)
    aps = {k[2:]: nc.dram_tensor(k, v.shape, mybir.dt.from_np(v.dtype), kind="ExternalInput").ap() for k, v in arrays.items()}
    out = nc.dram_tensor("d_out", (B, S, H), F32, kind="ExternalOutput").ap()
    build(nc, aps, out)
    r = run_bass_kernel_spmd(nc, [arrays], core_ids=[0])
    return r.results[0]["d_out"]
```

```python
from contextlib import ExitStack

import numpy as np

import concourse.bass as bass
from concourse import mybir

ALU = mybir.AluOpType
ACT = mybir.ActivationFunctionType
F32 = mybir.dt.float32
F16 = mybir.dt.float16
BF16 = mybir.dt.bfloat16
I32 = mybir.dt.int32
U32 = mybir.dt.uint32
AX = mybir.AxisListType

P = 128
B, S, H = 4, 256, 512
T, D = 64, 128
NCH = 2
CL = S // NCH
KT = H // P
HEADS, HD = 32, 16
I0, IT0 = 1792, 14
NE, EI = 16, 56
I1, IT1 = NE * EI, NE * EI // P
WSCALE = 256.0
J = 64
KW = 101
FCH = 10
TH = T // 2
NF = T
BIG = 1.0e30
EPS = 1e-5


def shape_constants():
    t = np.arange(TH)
    k = np.arange(KW) - KW // 2
    fwd, inv = np.zeros((P, TH)), np.zeros((P, TH))
    ker = np.zeros((3, P, KW))
    r = 0
    for m in range(NF // 2 + 1):
        w = 2 * np.pi * m / NF
        edge = m in (0, NF // 2)
        c = (1.0 if edge else 2.0) / NF
        cos, sin = np.cos, np.sin
        for fa, fb, fc, sign in ((cos, cos, cos, 1), (cos, sin, sin, -1), (sin, sin, cos, 1), (sin, cos, sin, 1)):
            fwd[r], inv[r] = fa(w * t), fb(w * t)
            for d in (-1, 0, 1):
                lag = k - TH * d
                ker[d + 1, r] = sign * c * fc(w * lag) * (np.abs(lag) < TH)
            r += 1
            if edge:
                break
    f32 = np.float32
    fwd4 = np.tile(fwd.T, (B, 1))
    fwd_hi = fwd4.astype(np.float16)
    bm = np.arange(P) // TH
    four = np.arange(B)[:, None]
    return {
        "c_ident": np.eye(P, dtype=f32),
        "c_fwd": np.stack([fwd_hi, (fwd4 - fwd_hi).astype(np.float16)], 1),
        "c_inv": inv.astype(f32),
        "c_ker": ker.transpose(2, 0, 1).astype(f32),
        "c_headsel": (np.arange(P)[:, None] // HD == np.arange(8)[None]).astype(f32),
        "c_expert": (np.arange(I1)[None] // EI == np.arange(NE)[:, None]).astype(f32),
        "c_iota": np.tile(np.arange(NE, dtype=f32), (P, 1)),
        "c_time": np.tile(np.arange(T, dtype=f32), (B, 1)),
        "c_time2": np.stack([np.tile(np.arange(TH), B), np.tile(np.arange(TH, T), B)]).astype(f32),
        "c_gatescale": np.stack([np.where(np.arange(P) < J, 1.0, 2.0), np.ones(P)], 1).astype(f32),
        "c_batchsel": (bm[None] == four).astype(f32),
        "c_half_batch": np.concatenate([np.repeat(np.eye(2), B, 1), np.tile(-2 * BIG * (np.arange(B)[None] != four), (1, 2))]).astype(f32),
    }


def build(nc, a, out):
    with ExitStack() as ctx:
        def sb(name, shape, dt=F32):
            return ctx.enter_context(nc.sbuf_tensor(name, shape, dt))

        def sem(name):
            return ctx.enter_context(nc.semaphore(name))

        x_sb = sb("x_sb", [P, NCH * B, H])
        xn = sb("xn", [P, 2, H])
        xT = sb("xT", [P, KT, B * CL])
        stats = sb("stats", [P, 2, 6])
        mv = sb("mv", [P, 2, 2])
        rstd = sb("rstd", [P, 2, 1])
        vareps = sb("vareps", [P, 2, 1])
        minus_half = sb("minus_half", [P, 1])
        krep = sb("krep", [P, KT, B, T])
        headsel = sb("headsel", [P, 8])
        kbd = sb("kbd", [P, 2, 512])
        vbd = sb("vbd", [P, B, 8, 34])
        mask_sb = sb("mask_sb", [P, NCH, T])
        smax = sb("smax", [P, 32])
        rsum = sb("rsum", [P, HEADS])
        wbig = sb("wbig", [P, 2 * KT * I0 + IT0 * H])
        sscale = sb("sscale", [P, 2, I0])
        interT = sb("interT", [P, IT0, B * CL])
        tanh_sb = sb("tanh_sb", [P, 2, 512])
        act_sb = sb("act_sb", [P, 2, 512])
        lys = sb("lys", [P, KT, 256])
        gbias = sb("gbias", [P, 2])
        gscale = sb("gscale", [P, 2])
        rin = sb("rin", [P, S, 8])
        ident = sb("ident", [P, P])
        identb = sb("identb", [P, P], BF16)
        ctxT = sb("ctxT", [P, 2, P])
        wahT = sb("wahT", [P, J])
        ba2 = sb("ba2", [P, 1])
        lgsT = sb("lgsT", [P, 256])
        lgyT = sb("lgyT", [P, J])
        lssT = sb("lssT", [J, 256])
        lss3 = sb("lss3", [J, 3, 256], BF16)
        lsyT = sb("lsyT", [J, J])
        wasT = sb("wasT", [J, P])
        was2 = sb("was2", [J, 2, P], F16)
        convw = sb("convw", [FCH, KW])
        wafT = sb("wafT", [FCH, J])
        va2 = sb("va2", [P, 1])
        vah = sb("vah", [P, 2, TH], BF16)
        vae = sb("vae", [P, 2, B])
        vae2 = sb("vae2", [P, 2, 2 * B], F16)
        fwd = sb("fwd", [P, 2, P], F16)
        inv = sb("inv", [P, TH])
        ker = sb("ker", [KW, 3, P])
        u_sb = sb("u_sb", [KW, J])
        uh = sb("uh", [P, 2, P])
        enc = sb("enc", [P, P])
        enc3 = sb("enc3", [P, 3, P], BF16)
        hg = sb("hg", [P, 2, 256])
        otmp = hg[:].rearrange("p h g -> p (h g)")
        hg2 = krep[:, 1:KT, :, :].rearrange("p k b t -> p (k b t)").bitcast(F16)[:, 0:1024].rearrange("p (j h g) -> p j h g", j=2, h=2)
        hy = sb("hy", [P, 2, J])
        onesb = sb("onesb", [P, P], BF16)
        lens = sb("lens", [B, 1], I32)
        lens2 = sb("lens2", [2, B], I32)
        lensf = sb("lensf", [B, 1])
        lens2f = sb("lens2f", [2, B])
        time = sb("time", [B, T])
        time2 = sb("time2", [2, P])
        bsel_f = sb("bsel_f", [B, P])
        etl_f = sb("etl_f", [2 + B, P])
        etr_f = sb("etr_f", [2 + B, 8])
        bsel = sb("bsel", [B, P], BF16)
        maskb = sb("maskb", [B, T], BF16)
        etl = sb("etl", [2 + B, P], BF16)
        etr = sb("etr", [2 + B, 8], BF16)
        bgy = sb("bgy", [J, 1])
        th = interT[:, 6, 0:P]
        th_hi = interT[:, 6, P:P + P // 2].bitcast(F16)
        th_lo = interT[:, 6, 2 * P:2 * P + P // 2].bitcast(F16)
        nmx = sb("nmx", [P, 1])
        eh = sb("eh", [P, 8], F16)
        el = sb("el", [P, 8], F16)
        ex = sb("ex", [P, 2, 8])
        rinv = sb("rinv", [P, 2, B])
        g1 = sb("g1", [P, 8])
        gat = sb("gat", [P, 8])
        rs = sb("rs", [P, 8])
        ahn = sb("ahn", [P, 8])
        sh = sb("sh", [J, B], F16)
        sl = sb("sl", [J, B], F16)
        qv = krep[:, 0, :, :].rearrange("p b t -> p (b t)").rearrange("p (i b t) -> p i b t", i=2, b=B)
        tfi = sb("tfi", [J, 8])
        xs = sb("xs", [J, 2, 12])
        ab = sb("ab", [J, 8])
        tc_sb = sb("tc_sb", [J, B])
        s2 = sb("s2", [J, 2, B])
        gwT = sb("gwT", [P, KT, NE])
        iota = sb("iota", [P, NE])

        reuse = sscale[:].rearrange("p a b -> p (a b)")
        ahist = reuse[:, 0:S * 8].rearrange("p (l b) -> p l b", b=8)
        shist = reuse[0:J, S * 8:S * 12].rearrange("p (l b) -> p l b", b=B)
        uT = reuse[0:J + 1, S * 12:S * 12 + B * CL].rearrange("p (b l) -> p b l", b=B)

        def in_tiles(ap, k):
            return ap.rearrange("p (k o) -> p k o", k=k)

        rin_free = rin[:].rearrange("p l b -> p (l b)").rearrange("p (g n) -> p g n", g=4)
        scores = [interT[:, 0:4, :], rin_free]
        pT = [interT[:, 4:6, :], reuse[:, 0:1024].rearrange("p (i n) -> p i n", i=2)]
        xT_tile = [interT[:, 13, :].rearrange("p (k t) -> p k t", k=KT), reuse[:, 1024:1536].rearrange("p (k t) -> p k t", k=KT)]
        xT_rec = [in_tiles(reuse[:, 512 * i:512 * (i + 1)], KT) for i in range(2)]
        more = interT[:, 6:13, :].rearrange("p a n -> p (a n)").rearrange("p (i n) -> p i n", i=2)
        scales = [sscale[:, 0, :], sscale[:, 1, :], more[:, 0, :], more[:, 1, :]]

        ahist2 = ahist.rearrange("p (i two) b -> p i two b", two=2)
        shist2 = shist.rearrange("p (i two) b -> p i two b", two=2)
        rin2 = rin[:].rearrange("p (i two) b -> p i two b", two=2)

        bank = [ctx.enter_context(nc.psum_tensor(f"bank{i}", [P, 512], F32)) for i in range(8)]

        nw = KT * I0
        words = wbig[:].bitcast(F16).rearrange("p (n two) -> p two n", two=2)

        wg, wu, wd = [[in_tiles(words[:, part, lo:hi], k) for part in (1, 0)]
                      for lo, hi, k in ((0, nw, KT), (nw, 2 * nw, KT), (2 * nw, 2 * nw + IT0 * H, IT0))]
        x_part = [in_tiles(xT[:].rearrange("p k t -> p (k t)").bitcast(F16)[:, i * KT * B * CL:(i + 1) * KT * B * CL], KT) for i in range(2)]
        i_part = [in_tiles(interT[:].rearrange("p k t -> p (k t)").bitcast(F16)[:, i * IT0 * B * CL:(i + 1) * IT0 * B * CL], IT0) for i in range(2)]
        m1 = KT * I1
        w1_places = ((0, m1, KT), (m1, 2 * m1, KT), (2 * m1, 3 * m1, IT1))
        w1_float = [in_tiles(wbig[:, lo:hi], k) for lo, hi, k in w1_places]
        w1g, w1u, w1d = [[in_tiles(words[:, part, lo:hi], k) for part in (1, 0)] for lo, hi, k in w1_places]
        place = [3 * m1]

        def behind(n, rows=P):
            place[0] += n
            return wbig[0:rows, place[0] - n:place[0]]

        expert = behind(I1, NE)
        lyy = behind(H, J + 1)
        expert_half = behind(I1 // 2, NE).bitcast(F16)
        wT_both = [behind(B * CL, NE).bitcast(F16) for c in range(NCH)]
        wT = [[both[:, i * B * CL:(i + 1) * B * CL] for i in range(2)] for both in wT_both]
        x1_part = []
        for c in range(NCH):
            both = behind(KT * B * CL).bitcast(F16)
            x1_part.append([in_tiles(both[:, i * KT * B * CL:(i + 1) * KT * B * CL], KT) for i in range(2)])
        lg = behind(B * NE).rearrange("p (b e) -> p b e", b=B)
        probs = behind(B * NE).rearrange("p (b e) -> p b e", b=B)
        top8 = behind(B * 8).rearrange("p (b e) -> p b e", b=B)
        idx8 = behind(B * 8).bitcast(U32).rearrange("p (b e) -> p b e", b=B)
        idxf = behind(B * 2).rearrange("p (b e) -> p b e", b=B)
        lmax = behind(B).unsqueeze(2)
        tsum = behind(B).unsqueeze(2)
        trec = behind(B).unsqueeze(2)
        wsel = behind(2 * B * NE).rearrange("p (j b e) -> p j b e", j=2, b=B)
        SPLIT0 = 16
        PIECE = 3 * m1 // (S // 2 - SPLIT0)
        assert PIECE * (S // 2 - SPLIT0) == 3 * m1
        piece_scaled = behind(PIECE)
        wscale = behind(1)
        piece_float = wbig[:, 0:3 * m1].rearrange("p (i n) -> p i n", n=PIECE)
        piece_part = [words[:, part, 0:3 * m1].rearrange("p (i n) -> p i n", n=PIECE) for part in (1, 0)]
        assert place[0] <= 2 * nw + IT0 * H

        names = """vareps_ready mv_ready rstd_ready attn_in values_in rec_in setup_in w1_in fin_in out_done
            ln_ready tr_done xT_ready chain pchain achain
            kbd_ready score_done sub_done exp_done pt_done pt_copied av_part attn_done
            product_ready high_ready low_ready low_odd xl_ready act_ready ih_ready gu_done th_done inter_done down_done x_added
            rec_done rin_ready
            vbd_zero setup_v setup_mm setup_cp mask_ready scale_ready
            pre_done th_s th_full th_lo_ready eb_done et_done mx_ready eh_ready ex_ready el_ready sum_done ah_done hg_done rinv_ready ahn_ready
            prod_ready g_ready q0_ready q1_ready kept tg_ready ab_ready c_ready tc_ready s_ready sh_ready sl_ready sp_done
            identb_ready hist_done part_ready
            split_scaled split_high split_done y_done u_ready yy_done lg_done lgx_ready pe_exp wsel_ready wt_done wT_ready wT_low_ready expert_ready""".split()
        s = {n: sem("s_" + n) for n in names}
        w_sc = [sem(f"s_scl{i}") for i in range(4)]
        w_in = [sem(f"s_w{i}") for i in range(9)]
        x_in = [sem(f"s_x{i}") for i in range(3)]

        block = ctx.enter_context(nc.Block())
        SETUP = 25
        DPART = [(0, 3), (3, 6), (6, 9), (9, 12), (12, 14)]
        LAST = 8 + len(DPART) - 1
        STEPS = 10

        def weight_slice(n):
            if n < 8:
                lo, size = n * I0, I0
            else:
                i0, i1 = DPART[n - 8]
                lo, size = 2 * nw + i0 * H, (i1 - i0) * H
            return (scales[n % 4][:, 0:size], wbig[:, lo:lo + size].bitcast(I32), words[:, 1, lo:lo + size], words[:, 0, lo:lo + size])

        def slices_at(k, g, lag):
            n = KT * (k - 1) + g - lag
            return [n] if 0 < k < B and n >= 0 else []

        def scores_of(k):
            return scores[k % 2 if k < B else 1]

        def ln_of(k):
            return k if k < B else B + k

        def attention_bank(k, kind, n):
            if k < B:
                return bank[2 * kind + n % 2]
            return bank[(k + (0, 1, 1 + KT)[kind] + (n % 4)) % 2]

        def chunk_steps(c, tile_steps):
            tiles = [tile_steps(c * B + b) for b in range(B)]
            for b in range(B):
                for j in range(STEPS):
                    if c == 0 and b > 0 and j < STEPS // 2:
                        continue
                    next(tiles[b])
                    yield
                    if c == 0 and b + 1 < B and j >= STEPS // 2:
                        next(tiles[b + 1])
                        yield

        @block.sync
        def _(sp):
            sp.dma_start(x_sb[:, 0, :], a["x"][0, 0:CL, :]).then_inc(x_in[0], 16)
            sp.dma_start(ident[:], a["c_ident"]).then_inc(s["attn_in"], 16)
            sp.dma_start(headsel[:], a["c_headsel"]).then_inc(s["attn_in"], 16)
            sp.dma_start(krep[:], a["krep"]).then_inc(s["attn_in"], 16)
            sp.dma_start(mask_sb[:], a["mask_SxS2_ff0"].rearrange("(c p) t -> p c t", p=P)).then_inc(s["values_in"], 16)
            sp.dma_start(x_sb[:, 1:B, :], a["x"][1:B, 0:CL, :].rearrange("b p h -> p b h")).then_inc(x_in[1], 16)
            sp.wait_ge(s["vbd_zero"], 1)
            for b in range(B):
                v = a["ctx_1024"][b].rearrange("t (g d) -> t g d", g=8)
                for h in range(2):
                    sp.dma_start(vbd[h * T:(h + 1) * T, b, :, h * 17:h * 17 + HD], v).then_inc(s["values_in"], 16)
            for n in range(8):
                src = a["gate_qT"] if n < 4 else a["up_qT"]
                sp.dma_start(weight_slice(n)[1], src[n % 4 * P:(n % 4 + 1) * P, :]).then_inc(w_in[n], 16)
                if n < 4:
                    sp.dma_start(scales[n], a["gate_sT"][n:n + 1, :].partition_broadcast(P)).then_inc(w_sc[n], 16)
            sp.dma_start(in_tiles(wbig[:, 2 * nw:], IT0).bitcast(I32), a["down_qT"].rearrange("(k p) o -> p k o", p=P)).then_inc(w_in[8], 16)
            sp.dma_start(x_sb[:, B:2 * B, :], a["x"][:, CL:2 * CL, :].rearrange("b p h -> p b h")).then_inc(x_in[2], 16)
            for n in range(4, 8 + len(DPART)):
                sp.wait_ge(s["low_odd" if n % 2 else "low_ready"], n // 2 - 1)
                if n < 8:
                    sp.dma_start(scales[n % 4], a["up_sT"][n % 4:n % 4 + 1, :].partition_broadcast(P)).then_inc(w_sc[n % 4], 16)
                else:
                    i0, i1 = DPART[n - 8]
                    sp.dma_start(scales[n % 4][:, 0:(i1 - i0) * H],
                                 a["down_sT"][i0:i1, :].rearrange("g h -> (g h)").unsqueeze(0).partition_broadcast(P)).then_inc(w_sc[n % 4], 16)
            sp.dma_start(lys[:], a["LysT"].rearrange("(k p) o -> p k o", p=P)).then_inc(s["rec_in"], 16)
            sp.dma_start(gbias[:], a["gsb2"]).then_inc(s["rec_in"], 16)
            sp.dma_start(gscale[:], a["c_gatescale"]).then_inc(s["rec_in"], 16)
            small_loads = [(ctxT[:], a["ctxT"]), (wahT[:], a["WahT"]), (lgsT[:], a["LgsT"]), (lgyT[:], a["LgyT"]),
                           (lssT[:], a["LssT"]), (lsyT[:], a["LsyT"]), (convw[:], a["convw"]),
                           (wafT[:], a["WafT"]), (fwd[:], a["c_fwd"]), (inv[:], a["c_inv"]), (ker[:], a["c_ker"]),
                           (lens[:], a["lens"]), (time[:], a["c_time"]), (time2[:], a["c_time2"]),
                           (bsel_f[:], a["c_batchsel"]), (etl_f[2:2 + B, :], a["c_batchsel"]), (etr_f[:], a["c_half_batch"])]
            for h in range(2):
                small_loads.append((ba2[h * J:(h + 1) * J, :], a["ba"]))
                small_loads.append((va2[h * J:(h + 1) * J, :], a["va"]))
                small_loads.append((wasT[:, h * J:(h + 1) * J], a["WasT"]))
                small_loads.append((lens2[h:h + 1, :], a["lens"].rearrange("b o -> o b")))
            assert len(small_loads) == SETUP
            for dst, src in small_loads:
                sp.dma_start(dst, src).then_inc(s["setup_in"], 16)
            for dst, src in ((bgy[:], a["bgy"]), (gwT[:], a["gwT"].rearrange("(k p) e -> p k e", p=P)), (iota[:], a["c_iota"])):
                sp.dma_start(dst, src).then_inc(s["fin_in"], 16)
            sp.wait_ge(s["down_done"], 2 * B)
            for dst, src in zip(w1_float, (a["g1T"], a["u1T"], a["d1T"])):
                sp.dma_start(dst, src.rearrange("(k p) o -> p k o", p=P)).then_inc(s["w1_in"], 16)
            for dst, src in ((expert, a["c_expert"]), (lyy[0:J, :], a["LyyT"]), (lyy[J:J + 1, :], a["byy"])):
                sp.dma_start(dst, src).then_inc(s["w1_in"], 16)
            for k in range(NCH * B):
                c, b = divmod(k, B)
                sp.wait_ge(s["x_added"], 4 * B + k + 1)
                sp.dma_start(out[b, c * CL:(c + 1) * CL, :], x_sb[:, k, :]).then_inc(s["out_done"], 16)
            sp.wait_ge(s["out_done"], 16 * NCH * B)

        @block.gpsimd
        def _(pool):
            nc.gpsimd.memset(vbd[:], 0.0).then_inc(s["pchain"], 1)
            nc.gpsimd.memset(onesb[:], 1.0)
            nc.gpsimd.memset(minus_half[:], -0.5)
            pool.wait_ge(s["pchain"], 1)
            nc.gpsimd.memset(vbd[0:T, :, :, 16:17], 1.0).then_inc(s["pchain"], 1)
            pool.wait_ge(s["pchain"], 2)
            nc.gpsimd.memset(vbd[T:P, :, :, 33:34], 1.0).then_inc(s["vbd_zero"], 1)

            def rstd_of(n):
                pool.wait_ge(s["mv_ready"], n + 1)
                nc.gpsimd.tensor_scalar(vareps[:, n % 2, :], mv[:, n % 2, 1:2], EPS, None, ALU.add).then_inc(s["vareps_ready"], 1)
                pool.wait_ge(s["vareps_ready"], n + 1)
                nc.gpsimd.tensor_tensor(rstd[:, n % 2, :], vareps[:, n % 2, :], minus_half[:], ALU.pow).then_inc(s["rstd_ready"], 1)

            def low_part(n):
                product, _, high, low = weight_slice(n)
                pool.wait_ge(s["high_ready"], n + 1)
                nc.gpsimd.tensor_tensor(low, product, high, ALU.subtract).then_inc(s["low_ready"], 1)

            def key_block(k, kt):
                n = k * KT + kt
                if n >= 2:
                    pool.wait_ge(s["score_done"], n - 1)
                nc.gpsimd.tensor_tensor(
                    kbd[:, n % 2, :].rearrange("p (h t) -> p h t", h=8),
                    krep[:, kt, k % B, :].unsqueeze(1).broadcast_to([P, 8, T]),
                    headsel[:].unsqueeze(2).broadcast_to([P, 8, T]), ALU.mult).then_inc(s["kbd_ready"], 1)

            def attention(k):
                key_block(k, 0)
                key_block(k, 1)
                yield
                for kt in range(KT):
                    if kt + 2 < KT:
                        key_block(k, kt + 2)
                    if kt == 2 and k % B + 1 < B:
                        rstd_of(ln_of(k + 1))
                    yield
                for g in range(4):
                    if k == B - 1 and g < 3:
                        rstd_of(B + g)
                    for n in slices_at(k, g, 2):
                        if n % 2 == 0:
                            low_part(n)
                    yield
                yield

            pool.wait_ge(s["vbd_zero"], 1)
            rstd_of(0)
            pool.wait_ge(s["attn_in"], 16 * 3)
            for _ in chunk_steps(0, attention):
                pass
            rstd_of(2 * B - 1)

            def hidden_low(base, tiles, other=None):
                for it in range(tiles):
                    n = base + it
                    if other is not None:
                        for _ in range(6 if it == 0 else 3):
                            next(other, None)
                    pool.wait_ge(s["ih_ready"], n + 1)
                    nc.gpsimd.tensor_tensor(i_part[1][:, it, :], act_sb[:, n % 2, :], i_part[0][:, it, :], ALU.subtract).then_inc(s["inter_done"], 1)

            rstd_of(2 * B)
            low_part(LAST - 2)
            low_part(LAST)
            hidden_low(0, IT0, chunk_steps(1, attention))
            for j in range(3 * B, 5 * B):
                rstd_of(j)
            pool.wait_ge(s["setup_in"], 16 * SETUP)
            nc.gpsimd.tensor_scalar(lssT[:, 0:J], lssT[:, 0:J], 0.5, None, ALU.mult)
            nc.gpsimd.tensor_scalar(lssT[:, 2 * J:4 * J], lssT[:, 2 * J:4 * J], 0.5, None, ALU.mult)
            nc.gpsimd.tensor_scalar(lsyT[:], lsyT[:], 0.5, None, ALU.mult)
            nc.gpsimd.tensor_scalar(wasT[:], wasT[:], 0.5, None, ALU.mult)
            nc.gpsimd.tensor_scalar(lgsT[:, J:2 * J], lgsT[:, J:2 * J], 2.0, None, ALU.mult).then_inc(s["scale_ready"], 1)
            nc.gpsimd.memset(xs[:], 0.0)
            nc.gpsimd.memset(s2[:], 0.0).then_inc(s["s_ready"], 1)
            nc.gpsimd.memset(sh[:], 0.0).then_inc(s["sh_ready"], 1)
            nc.gpsimd.memset(sl[:], 0.0).then_inc(s["sl_ready"], 1)
            nc.gpsimd.memset(vah[:], 0.0)
            nc.gpsimd.memset(vae[:], 0.0).then_inc(s["pchain"], 1)
            pool.wait_ge(s["pchain"], 3)
            nc.gpsimd.memset(uT[J:J + 1, :, :], 1.0).then_inc(s["pchain"], 1)
            pool.wait_ge(s["pchain"], 4)
            nc.gpsimd.tensor_copy(vah[0:J, 0, :], va2[0:J, 0:1].broadcast_to([J, TH]))
            nc.gpsimd.tensor_copy(vae[0:J, 0, :], va2[0:J, 0:1].broadcast_to([J, B])).then_inc(s["pchain"], 1)
            pool.wait_ge(s["pchain"], 5)
            nc.gpsimd.tensor_copy(vah[J:P, 1, :], va2[J:P, 0:1].broadcast_to([J, TH]))
            nc.gpsimd.tensor_copy(vae[J:P, 1, :], va2[J:P, 0:1].broadcast_to([J, B])).then_inc(s["setup_v"], 1)
            pool.wait_ge(s["setup_v"], 1)
            nc.gpsimd.tensor_copy(identb[:], ident[:]).then_inc(s["identb_ready"], 1)

            hidden_low(IT0, IT0)
            for j in range(5 * B, 6 * B):
                rstd_of(j)

            def keep(i, par):
                l = i * 2 + par
                pool.wait_ge(s["s_ready"], l + 1)
                nc.gpsimd.tensor_copy(shist2[:, bass.ds(i, 1), par, :], s2[:, par:par + 1, :]).then_inc(s["kept"], 1)
                pool.wait_ge(s["rinv_ready"], l + 1)
                nc.gpsimd.tensor_tensor(ahist2[:, bass.ds(i, 1), par, :].rearrange("p one (o b) -> p (one o) b", o=2),
                                        ex[:, par, :].rearrange("p (o b) -> p o b", o=2),
                                        rinv[:, par:par + 1, :].broadcast_to([P, 2, B]), ALU.mult).then_inc(s["hist_done"], 1)

            with pool.Fori(0, SPLIT0) as i:
                for par in range(2):
                    keep(i, par)
            pool.wait_ge(s["w1_in"], 96)
            nc.gpsimd.tensor_copy(expert_half, expert).then_inc(s["expert_ready"], 1)
            pool.wait_ge(s["expert_ready"], 1)
            nc.gpsimd.memset(wscale, WSCALE).then_inc(s["split_scaled"], 1)
            nc.gpsimd.memset(piece_scaled, 0.0).then_inc(s["split_done"], 1)
            pool.wait_ge(s["split_scaled"], 1)
            with pool.Fori(SPLIT0, S // 2) as i:
                keep(i, 0)
                piece = i - SPLIT0
                pool.wait_ge(s["split_done"], piece + 1)
                nc.gpsimd.tensor_tensor(piece_scaled.unsqueeze(1), piece_float[:, bass.ds(piece, 1), :],
                                        wscale.unsqueeze(2).broadcast_to([P, 1, PIECE]), ALU.mult).then_inc(s["split_scaled"], 1)
                pool.wait_ge(s["split_scaled"], piece + 2)
                nc.gpsimd.tensor_copy(piece_part[0][:, bass.ds(piece, 1), :], piece_scaled.unsqueeze(1)).then_inc(s["split_high"], 1)
                keep(i, 1)
                pool.wait_ge(s["split_high"], piece + 1)
                nc.gpsimd.tensor_tensor(piece_part[1][:, bass.ds(piece, 1), :], piece_scaled.unsqueeze(1),
                                        piece_part[0][:, bass.ds(piece, 1), :], ALU.subtract).then_inc(s["split_done"], 1)

            def prelude(c):
                yield
                for b in range(B):
                    rstd_of(6 * B + c * B + b)
                    yield
                for b in range(B):
                    cols = slice(b * CL, (b + 1) * CL)
                    pool.wait_ge(s["xT_ready"], 6 * B + c * B + b + 1)
                    nc.gpsimd.tensor_tensor(x1_part[c][1][:, :, cols], xT[:, :, cols], x1_part[c][0][:, :, cols], ALU.subtract).then_inc(s["xl_ready"], 1)
                    yield
                yield
                yield

            for _ in prelude(0):
                pass
            hidden_low(2 * IT0, IT1, prelude(1))
            hidden_low(2 * IT0 + IT1, IT1)

        @block.vector
        def _(dve):
            chain = [0]

            def link(ins):
                chain[0] += 1
                ins.then_inc(s["chain"], 1)
                dve.wait_ge(s["chain"], chain[0])

            def moments(n, k):
                q = n % 2
                link(nc.vector.bn_stats(stats[:, q, :], x_sb[:, k, :]))
                nc.vector.bn_aggr(mv[:, q, :], stats[:, q, :]).then_inc(s["mv_ready"], 1)

            def normalise(n, k):
                q = n % 2
                if n >= 2:
                    dve.wait_ge(s["tr_done"], n - 1)
                dve.wait_ge(s["rstd_ready"], n + 1)
                nc.vector.tensor_scalar(xn[:, q, :], x_sb[:, k, :], mv[:, q, 0:1], rstd[:, q, 0:1],
                                        ALU.subtract, ALU.mult).then_inc(s["ln_ready"], 1)

            def layernorm(n, k):
                moments(n, k)
                normalise(n, k)

            def layernorms(n, tiles, after=None):
                moments(n, tiles[0])
                for i, k in enumerate(tiles):
                    if i + 1 < len(tiles):
                        moments(n + i + 1, tiles[i + 1])
                    normalise(n + i, k)
                    if after is not None:
                        after(i)

            def dequantise(n):
                product, integers, _, _ = weight_slice(n)
                dve.wait_ge(w_in[min(n, 8)], 16)
                dve.wait_ge(w_sc[n % 4], 16 * (n // 4 + 1))
                nc.vector.scalar_tensor_tensor(product, integers, WSCALE, product, ALU.mult, ALU.mult).then_inc(s["product_ready"], 1)

            def low_part(n):
                product, _, high, low = weight_slice(n)
                dve.wait_ge(s["high_ready"], n + 1)
                nc.vector.tensor_tensor(low, product, high, ALU.subtract).then_inc(s["low_odd"], 1)

            def input_low(n, b):
                dve.wait_ge(s["xT_ready"], n + 1)
                nc.vector.tensor_tensor(x_part[1][:, :, b * CL:(b + 1) * CL], bank[n % 2][:].rearrange("p (k t) -> p k t", k=KT),
                                        x_part[0][:, :, b * CL:(b + 1) * CL], ALU.subtract).then_inc(s["xl_ready"], 1)

            def attention(k):
                c, b = divmod(k, B)
                sc = scores_of(k)
                yield
                for kt in range(KT):
                    n = k * KT + kt
                    dve.wait_ge(s["score_done"], n + 1)
                    before = k - (2 if c == 0 else 1)
                    if kt == 0 and before >= 0:
                        dve.wait_ge(s["pt_done"], 4 * (before + 1))
                    v = sc[:, kt, :].rearrange("p (h t) -> p h t", h=8)
                    link(nc.vector.scalar_tensor_tensor(
                        v, attention_bank(k, 1, n)[:].rearrange("p (h t) -> p h t", h=8), 0.25,
                        mask_sb[:, c:c + 1, :].broadcast_to([P, 8, T]), ALU.mult, ALU.add))
                    sc_max = smax[:, kt * 8:(kt + 1) * 8]
                    link(nc.vector.tensor_reduce(sc_max, v, AX.X, ALU.max))
                    nc.vector.tensor_tensor(v, v, sc_max.unsqueeze(2).broadcast_to([P, 8, T]), ALU.subtract).then_inc(s["sub_done"], 1)
                    if kt == 2 and b + 1 < B:
                        layernorm(ln_of(k + 1), k + 1)
                    yield
                for g in range(4):
                    if k == B - 1 and g < 3:
                        moments(B + g, g)
                    for n in slices_at(k, g, 0):
                        dequantise(n)
                    if k == B - 1 and g < 3:
                        normalise(B + g, g)
                    if k == B - 1 and g > 1:
                        input_low(B + g - 2, g - 2)
                    for n in slices_at(k, g, 2):
                        if n % 2 == 1:
                            low_part(n)
                    yield
                if k == B - 1:
                    input_low(B + 2, 2)
                dve.wait_ge(s["av_part"], 4 * (k + 1))
                for h in range(2):
                    o = bank[6 + h][:, 0:272].rearrange("p (h e) -> p h e", e=17)
                    r = rsum[:, 16 * h:16 * h + 16]
                    link(nc.vector.reciprocal(r.unsqueeze(2), o[:, :, 16:17]))
                    link(nc.vector.tensor_tensor(otmp[:, 256 * h:256 * h + 256].rearrange("p (h d) -> p h d", d=HD), o[:, :, 0:HD],
                                                 r.unsqueeze(2).broadcast_to([P, 16, HD]), ALU.mult))
                nc.vector.tensor_tensor(x_sb[:, k, :], x_sb[:, k, :], otmp, ALU.add).then_inc(s["attn_done"], 1)
                dve.wait_ge(s["attn_done"], k + 1)
                yield

            def swiglu(base, tiles, expert_weights, other=None):
                for it in range(tiles):
                    n = base + it
                    if other is not None:
                        for _ in range(3):
                            next(other, None)
                    dve.wait_ge(s["th_done"], n + 1)
                    q = n % 2
                    if n >= 2:
                        dve.wait_ge(s["inter_done"], n - 1)
                    link(nc.vector.scalar_tensor_tensor(act_sb[:, q, :], tanh_sb[:, q, :], 1.0, bank[2 + q][:], ALU.add, ALU.mult))
                    scaled = nc.vector.scalar_tensor_tensor(act_sb[:, q, :], act_sb[:, q, :], 0.5 / WSCALE ** 2, bank[4 + q][:], ALU.mult, ALU.mult)
                    if expert_weights:
                        link(scaled)
                        nc.vector.tensor_tensor(act_sb[:, q, :], act_sb[:, q, :], bank[q][:], ALU.mult).then_inc(s["act_ready"], 1)
                    else:
                        scaled.then_inc(s["act_ready"], 1)

            added = [0]

            def add_residual(k, bk, ready, count, scale=1.0):
                dve.wait_ge(ready, count)
                added[0] += 1
                nc.vector.scalar_tensor_tensor(x_sb[:, k, :], bk[:], scale, x_sb[:, k, :], ALU.mult, ALU.add).then_inc(s["x_added"], 1)
                dve.wait_ge(s["x_added"], added[0])

            dve.wait_ge(x_in[0], 16)
            layernorm(0, 0)
            dve.wait_ge(x_in[1], 16)
            dve.wait_ge(s["values_in"], 16 * 9)
            for _ in chunk_steps(0, attention):
                pass
            dequantise(LAST)
            dve.wait_ge(x_in[2], 16)
            layernorms(2 * B - 1, [B - 1, B])
            input_low(2 * B - 1, B - 1)
            low_part(LAST - 1)
            swiglu(0, IT0, False, chunk_steps(1, attention))
            layernorms(3 * B, [B, B + 1, B + 2, B + 3], lambda i: input_low(3 * B + i - 1, i - 1) if 0 < i < 3 else None)
            for b in range(B):
                add_residual(b, bank[6 + b % 2], s["down_done"], b + 1, 1 / WSCALE)
                if b < 2:
                    input_low(3 * B + 2 + b, 2 + b)
            layernorms(4 * B, [0, 1, 2, 3])

            dve.wait_ge(s["setup_in"], 16 * SETUP)
            nc.vector.tensor_copy(lensf[:], lens[:])
            link(nc.vector.tensor_copy(lens2f[:], lens2[:]))
            nc.vector.tensor_scalar(maskb[:], time[:], lensf[:, 0:1], -BIG, ALU.is_ge, ALU.mult)
            link(nc.vector.tensor_tensor(time2[:].rearrange("p (b t) -> p b t", b=B), time2[:].rearrange("p (b t) -> p b t", b=B),
                                         lens2f[:].unsqueeze(2).broadcast_to([2, B, TH]), ALU.is_ge))
            link(nc.vector.tensor_scalar(etl_f[0:2, :], time2[:], -BIG, None, ALU.mult))
            nc.vector.tensor_copy(etl[:], etl_f[:])
            nc.vector.tensor_copy(etr[:], etr_f[:])
            nc.vector.tensor_copy(bsel[:], bsel_f[:]).then_inc(s["mask_ready"], 1)

            def in_halves(dst, src):
                link(nc.vector.tensor_copy(dst[:, 0], src))
                nc.vector.tensor_tensor(dst[:, 1], src, dst[:, 0], ALU.subtract).then_inc(s["part_ready"], 1)

            def in_parts(dst, src):
                for j in range(2):
                    link(nc.vector.tensor_copy(dst[:, j], src))
                    link(nc.vector.tensor_tensor(src, src, dst[:, j], ALU.subtract))
                nc.vector.tensor_copy(dst[:, 2], src).then_inc(s["part_ready"], 1)

            def context_parts():
                for _ in range(3 * (IT0 - 4)):
                    yield
                dve.wait_ge(s["setup_cp"], 2)
                in_parts(enc3[:], enc[:])
                in_halves(hg2, hg[:])
                yield

            dve.wait_ge(s["scale_ready"], 1)
            in_parts(lss3[:], lssT[:])
            in_halves(was2[:], wasT[:])
            dve.wait_ge(s["setup_v"], 1)
            in_halves(vae2[:], vae[:].rearrange("p h b -> p (h b)"))
            swiglu(IT0, IT0, False, context_parts())
            for b in range(B):
                add_residual(B + b, bank[6 + b % 2], s["down_done"], B + b + 1, 1 / WSCALE)
                layernorm(5 * B + b, B + b)

            def by_half(ap):
                return ap.rearrange("p (o b) -> p o b", o=2)

            with dve.Fori(0, S // 2) as i:
                for par in range(2):
                    l = i * 2 + par
                    dve.wait_ge(s["sp_done"], l + 1)
                    nc.vector.tensor_tensor(rs[:].unsqueeze(1), bank[6][:, 0:8].unsqueeze(1), rin2[:, bass.ds(i, 1), par, :], ALU.add)
                    dve.wait_ge(s["th_full"], l + 1)
                    nc.vector.tensor_tensor(th_lo, th, th_hi, ALU.subtract).then_inc(s["th_lo_ready"], 1)
                    dve.wait_ge(s["eb_done"], l + 1)
                    nc.vector.tensor_reduce(nmx[:], bank[2][:, 0:T], AX.X, ALU.max, negate=True).then_inc(s["mx_ready"], 1)
                    dve.wait_ge(s["ex_ready"], l + 1)
                    nc.vector.tensor_tensor(el[:], ex[:, par, :], eh[:], ALU.subtract).then_inc(s["el_ready"], 1)
                    dve.wait_ge(s["sum_done"], l + 1)
                    nc.vector.reciprocal(rinv[:, par, :], bank[5][:, 8:12]).then_inc(s["rinv_ready"], 1)
                    norm = rinv[:, par:par + 1, :].broadcast_to([P, 2, B])
                    dve.wait_ge(s["rinv_ready"], l + 1)
                    dve.wait_ge(s["hg_done"], l + 1)
                    nc.vector.tensor_tensor(by_half(g1[:]), by_half(bank[4][:, 0:8]), norm, ALU.mult).then_inc(s["prod_ready"], 1)

                    def spread(h):
                        return nc.vector.tensor_tensor(qv[:, h, :, :], inv[:].unsqueeze(1).broadcast_to([P, B, TH]),
                                                       ahn[:, 4 * h:4 * h + 4].unsqueeze(2).broadcast_to([P, B, TH]), ALU.mult)

                    dve.wait_ge(s["ah_done"], l + 1)
                    nc.vector.tensor_tensor(by_half(ahn[:]), by_half(bank[7][:, 0:8]), norm, ALU.mult).then_inc(s["ahn_ready"], 1)
                    dve.wait_ge(s["prod_ready"], l + 1)
                    nc.vector.tensor_tensor(gat[:], g1[:], rs[:], ALU.add).then_inc(s["g_ready"], 1)
                    dve.wait_ge(s["ahn_ready"], l + 1)
                    spread(0).then_inc(s["q0_ready"], 1)
                    dve.wait_ge(s["kept"], l + 1)
                    spread(1).then_inc(s["q1_ready"], 1)
                    dve.wait_ge(s["tg_ready"], l + 1)
                    nc.vector.scalar_tensor_tensor(ab[:], tfi[:], 1.0, xs[:, par, 0:8], ALU.add, ALU.mult).then_inc(s["ab_ready"], 1)
                    dve.wait_ge(s["ab_ready"], l + 1)
                    nc.vector.scalar_tensor_tensor(xs[:, 1 - par, 0:4], ab[:, 0:4], 0.5, ab[:, 4:8], ALU.mult, ALU.add).then_inc(s["c_ready"], 1)
                    dve.wait_ge(s["tc_ready"], l + 1)
                    nc.vector.scalar_tensor_tensor(sh[:], xs[:, par, 8:12], 1.0, tc_sb[:], ALU.add, ALU.mult).then_inc(s["sh_ready"], 1)
                    nc.vector.scalar_tensor_tensor(s2[:, 1 - par, :], xs[:, par, 8:12], 1.0, tc_sb[:], ALU.add, ALU.mult).then_inc(s["s_ready"], 1)
                    dve.wait_ge(s["s_ready"], l + 2)
                    nc.vector.tensor_tensor(sl[:], s2[:, 1 - par, :], sh[:], ALU.subtract).then_inc(s["sl_ready"], 1)


            def prelude(c):
                yield
                for b in range(B):
                    k = c * B + b
                    add_residual(k, bank[6 + (b + 1) % 2], s["yy_done"], k + 1)
                    moments(6 * B + k, k)
                    if b > 0:
                        normalise(6 * B + k - 1, k - 1)
                    yield
                normalise(6 * B + k, k)
                for b in range(B):
                    yield
                dve.wait_ge(s["lg_done"], c + 1)
                logits = bank[7][:, 0:B * NE].rearrange("p (b e) -> p b e", b=B)
                link(nc.vector.tensor_reduce(lmax, logits, AX.X, ALU.max))
                nc.vector.tensor_tensor(lg, logits, lmax.broadcast_to([P, B, NE]), ALU.subtract).then_inc(s["lgx_ready"], 1)
                dve.wait_ge(s["pe_exp"], c + 1)
                for b in range(B):
                    ins = nc.vector.max(top8[:, b, :], probs[:, b, :])
                link(ins)
                nc.vector.tensor_tensor(tsum, top8[:, :, 0:1], top8[:, :, 1:2], ALU.add)
                for b in range(B):
                    ins = nc.vector.max_index(idx8[:, b, :], top8[:, b, :], probs[:, b, :])
                link(ins)
                nc.vector.reciprocal(trec, tsum)
                link(nc.vector.tensor_copy(idxf, idx8[:, :, 0:2]))
                nc.vector.tensor_tensor(top8[:, :, 0:2], top8[:, :, 0:2], trec.broadcast_to([P, B, 2]), ALU.mult)
                if c > 0:
                    dve.wait_ge(s["wt_done"], c)
                for j in range(2):
                    ins = nc.vector.tensor_tensor(wsel[:, j], iota[:].unsqueeze(1).broadcast_to([P, B, NE]),
                                                  idxf[:, :, j:j + 1].broadcast_to([P, B, NE]), ALU.is_equal)
                link(ins)
                for j in range(2):
                    ins = nc.vector.tensor_tensor(wsel[:, j], wsel[:, j], top8[:, :, j:j + 1].broadcast_to([P, B, NE]), ALU.mult)
                link(ins)
                nc.vector.tensor_tensor(wsel[:, 0], wsel[:, 0], wsel[:, 1], ALU.add).then_inc(s["wsel_ready"], 1)
                yield
                dve.wait_ge(s["wT_ready"], c + 1)
                nc.vector.tensor_tensor(wT[c][1], bank[6][0:NE, :], wT[c][0], ALU.subtract).then_inc(s["wT_low_ready"], 1)
                yield

            for _ in prelude(0):
                pass
            for c in range(NCH):
                swiglu(2 * IT0 + c * IT1, IT1, True, prelude(1) if c == 0 else None)
                for b in range(B):
                    k = c * B + b
                    add_residual(k, bank[6 + b % 2], s["down_done"], 2 * B + k + 1, 1 / WSCALE)

        @block.scalar
        def _(act):
            def copy_xT(n, b):
                act.wait_ge(s["tr_done"], n + 1)
                nc.scalar.activation(x_part[0][:, :, b * CL:(b + 1) * CL], bank[n % 2][:].rearrange("p (k t) -> p k t", k=KT), ACT.Copy).then_inc(s["xT_ready"], 1)

            def high_part(n):
                product, _, high, _ = weight_slice(n)
                act.wait_ge(s["product_ready"], n + 1)
                nc.scalar.activation(high, product, ACT.Copy).then_inc(s["high_ready"], 1)

            def attention(k):
                c, b = divmod(k, B)
                n = ln_of(k)
                act.wait_ge(s["tr_done"], n + 1)
                if b > 0:
                    act.wait_ge(s["score_done"], KT * k)
                nc.scalar.activation(xT_tile[c],
                                     attention_bank(k, 0, n)[:].rearrange("p (k t) -> p k t", k=KT), ACT.Copy).then_inc(s["xT_ready"], 1)
                yield
                sc = scores_of(k)
                for kt in range(KT):
                    act.wait_ge(s["sub_done"], k * KT + kt + 1)
                    nc.scalar.activation(sc[:, kt, :], sc[:, kt, :], ACT.Exp).then_inc(s["exp_done"], 1)
                    yield
                for g in range(4):
                    n = 4 * k + g
                    act.wait_ge(s["pt_done"], n + 1)
                    if n >= 2:
                        act.wait_ge(s["av_part"], n - 1)
                    nc.scalar.activation(pT[c][:, n % 2, :], attention_bank(k, 2, n)[:], ACT.Copy).then_inc(s["pt_copied"], 1)
                    for n in slices_at(k, g, 1):
                        high_part(n)
                    if k == B - 1 and g > 0:
                        copy_xT(B + g - 1, g - 1)
                    yield
                yield

            def hidden_high(n, it):
                act.wait_ge(s["act_ready"], n + 1)
                nc.scalar.activation(i_part[0][:, it, :], act_sb[:, n % 2, :], ACT.Copy).then_inc(s["ih_ready"], 1)

            def tanh_gate(base, tiles, other=None):
                for it in range(tiles):
                    n = base + it
                    if other is not None:
                        for _ in range(3):
                            next(other, None)
                    act.wait_ge(s["gu_done"], n + 1)
                    if n >= 2:
                        act.wait_ge(s["act_ready"], n - 1)
                    nc.scalar.activation(tanh_sb[:, n % 2, :], bank[2 + n % 2][:], ACT.Tanh, scale=0.5 / WSCALE).then_inc(s["th_done"], 1)
                    if it > 0:
                        hidden_high(n - 1, it - 1)
                hidden_high(base + tiles - 1, tiles - 1)

            for _ in chunk_steps(0, attention):
                pass
            high_part(LAST - 1)
            high_part(LAST)

            def gates_input(c, b):
                k = c * B + b
                n = 4 * B + k
                act.wait_ge(s["tr_done"], n + 1)
                if k >= 2:
                    act.wait_ge(s["rec_done"], k - 1)
                nc.scalar.activation(xT_rec[k % 2], bank[n % 2][:].rearrange("p (k t) -> p k t", k=KT), ACT.Copy).then_inc(s["xT_ready"], 1)
                yield
                act.wait_ge(s["rec_done"], k + 1)
                for gp in range(2):
                    last = nc.scalar.activation(rin[:, c * CL:(c + 1) * CL, gp * B + b:gp * B + b + 1],
                                                bank[(6 if c == 0 else 2) + b % 2][:, gp * CL:(gp + 1) * CL].unsqueeze(2), ACT.Identity,
                                                bias=gbias[:, gp:gp + 1], scale=gscale[:, gp:gp + 1])
                last.then_inc(s["rin_ready"], 1)
                yield

            def between():
                for b in range(B):
                    yield from gates_input(0, b)
                act.wait_ge(s["setup_mm"], 1)
                act.wait_ge(s["setup_in"], 16 * SETUP)
                nc.scalar.activation(u_sb[:], bank[7][0:KW, 0:J], ACT.Copy)
                nc.scalar.activation(enc[:], bank[7][:, J:J + P], ACT.Identity, bias=ba2[:, 0:1])
                nc.scalar.activation(hy[:], bank[7][:, J + P:J + 2 * P].rearrange("p (h g) -> p h g", h=2), ACT.Copy)
                nc.scalar.activation(hg[:], bank[6][:].rearrange("p (h g) -> p h g", h=2), ACT.Copy).then_inc(s["setup_cp"], 1)
                yield
                act.wait_ge(s["setup_mm"], 2)
                nc.scalar.activation(uh[:], bank[6][:, 0:256].rearrange("p (h g) -> p h g", h=2), ACT.Copy).then_inc(s["setup_cp"], 1)
                yield

            copy_xT(2 * B - 1, B - 1)
            tanh_gate(0, IT0, chunk_steps(1, attention))
            for b in range(B):
                copy_xT(3 * B + b, b)
            act.wait_ge(s["rec_in"], 48)
            for gp in range(2):
                last = nc.scalar.activation(gbias[:, gp:gp + 1], gbias[:, gp:gp + 1], ACT.Copy, scale=gscale[:, gp:gp + 1])
            last.then_inc(s["achain"], 1)
            act.wait_ge(s["achain"], 1)
            tanh_gate(IT0, IT0, between())
            for b in range(B):
                for _ in gates_input(1, b):
                    pass

            with act.Fori(0, S // 2) as i:
                for par in range(2):
                    l = i * 2 + par
                    act.wait_ge(s["pre_done"], l + 1)
                    nc.scalar.activation(th_hi, bank[par][:, 0:P], ACT.Tanh).then_inc(s["th_s"], 1)
                    nc.scalar.activation(th, bank[par][:, 0:P], ACT.Tanh).then_inc(s["th_full"], 1)
                    act.wait_ge(s["et_done"], l + 1)
                    act.wait_ge(s["mx_ready"], l + 1)
                    nc.scalar.activation(eh[:], bank[3][:, 0:8], ACT.Exp, bias=nmx[:, 0:1]).then_inc(s["eh_ready"], 1)
                    nc.scalar.activation(ex[:, par, :], bank[3][:, 0:8], ACT.Exp, bias=nmx[:, 0:1]).then_inc(s["ex_ready"], 1)
                    act.wait_ge(s["g_ready"], l + 1)
                    nc.scalar.activation(xs[:, par, 4:12], gat[J:P, :], ACT.Tanh, scale=0.5)
                    nc.scalar.activation(tfi[:], gat[0:J, :], ACT.Tanh, scale=0.5).then_inc(s["tg_ready"], 1)
                    act.wait_ge(s["c_ready"], l + 1)
                    nc.scalar.activation(tc_sb[:], xs[:, 1 - par, 0:4], ACT.Tanh, scale=0.5).then_inc(s["tc_ready"], 1)

            act.wait_ge(s["fin_in"], 48)

            def prelude(c):
                act.wait_ge(s["y_done"], c + 1)
                if c > 0:
                    act.wait_ge(s["yy_done"], B * c)
                nc.scalar.activation(uT[0:J, :, :], bank[6][0:J, :].rearrange("p (l b) -> p b l", b=B),
                                     ACT.Tanh, bias=bgy[:, 0:1]).then_inc(s["u_ready"], 1)
                yield
                for b in range(B):
                    yield
                if c > 0:
                    act.wait_ge(s["lg_done"], c)
                for b in range(B):
                    act.wait_ge(s["tr_done"], 6 * B + c * B + b + 1)
                    for dst in (xT, x1_part[c][0]):
                        last = nc.scalar.activation(dst[:, :, b * CL:(b + 1) * CL], bank[6 + (b + 1) % 2][:].rearrange("p (k t) -> p k t", k=KT), ACT.Copy)
                    last.then_inc(s["xT_ready"], 1)
                    yield
                act.wait_ge(s["lgx_ready"], c + 1)
                nc.scalar.activation(probs, lg, ACT.Exp).then_inc(s["pe_exp"], 1)
                yield
                act.wait_ge(s["wt_done"], c + 1)
                nc.scalar.activation(wT[c][0], bank[6][0:NE, :], ACT.Copy).then_inc(s["wT_ready"], 1)
                yield

            for _ in prelude(0):
                pass
            for c in range(NCH):
                tanh_gate(2 * IT0 + c * IT1, IT1, prelude(1) if c == 0 else None)

        @block.tensor
        def _(pe):
            mm = nc.tensor.matmul

            def transposes(n):
                pe.wait_ge(s["ln_ready"], n + 1)
                if n >= 2:
                    pe.wait_ge(s["xT_ready"], n - 1)
                for kt in range(KT):
                    last = nc.tensor.transpose(bank[n % 2][:, kt * P:(kt + 1) * P], xn[:, n % 2, kt * P:(kt + 1) * P], ident[:])
                last.then_inc(s["tr_done"], 1)

            def attention(k):
                c, b = divmod(k, B)
                n_ln = ln_of(k)
                pe.wait_ge(s["ln_ready"], n_ln + 1)
                if n_ln >= 2:
                    pe.wait_ge(s["xT_ready"], n_ln - 1)
                for kt in range(KT):
                    last = nc.tensor.transpose(attention_bank(k, 0, n_ln)[:, kt * P:(kt + 1) * P], xn[:, n_ln % 2, kt * P:(kt + 1) * P], ident[:])
                last.then_inc(s["tr_done"], 1)
                yield
                pe.wait_ge(s["xT_ready"], n_ln + 1)
                for kt in range(KT):
                    n = k * KT + kt
                    pe.wait_ge(s["kbd_ready"], n + 1)
                    if n >= 2:
                        pe.wait_ge(s["sub_done"], n - 1)
                    mm(attention_bank(k, 1, n)[:], xT_tile[c][:, kt, :], kbd[:, n % 2, :],
                       start=True, stop=True).then_inc(s["score_done"], 1)
                    yield
                sc = scores_of(k)
                for g in range(5):
                    if g < 4:
                        n = 4 * k + g
                        pe.wait_ge(s["exp_done"], n + 1)
                        if c == 1 and g < 2:
                            pe.wait_ge(s["sub_done"], KT * k + 3 + g)
                        if n >= 2:
                            pe.wait_ge(s["pt_copied"], n - 1)
                        for j in range(4):
                            last = nc.tensor.transpose(attention_bank(k, 2, n)[:, j * P:(j + 1) * P], sc[:, g, j * P:(j + 1) * P], ident[:])
                        last.then_inc(s["pt_done"], 1)
                    if g >= 1:
                        n = 4 * k + g - 1
                        pe.wait_ge(s["pt_copied"], n + 1)
                        if g == 1 and k > 0:
                            pe.wait_ge(s["attn_done"], k)
                        if g == 1 and k == 0:
                            pe.wait_ge(s["values_in"], 16 * 9)
                        for j in range(4):
                            p = 4 * (g - 1) + j
                            last = mm(bank[6 + p // 8][:, (p % 8) * 34:(p % 8) * 34 + 34], pT[c][:, n % 2, j * P:(j + 1) * P],
                                      vbd[:, b, p // 2, :], start=True, stop=True)
                        last.then_inc(s["av_part"], 1)
                    if k == B - 1 and 0 < g < 4:
                        input_transposes(B + g - 1, g - 1)
                    yield

            def gate_up(base, tiles, g, u, x, weights=None, other=None):
                for it in range(tiles):
                    n = base + it
                    if n >= 2:
                        pe.wait_ge(s["act_ready"], n - 1)
                    if weights is not None:
                        for wi in range(2):
                            mm(bank[n % 2][:], expert_half[:, it * P:(it + 1) * P], weights[wi], start=(wi == 0), stop=(wi == 1))
                    for w, bk in ((g, bank[2 + n % 2]), (u, bank[4 + n % 2])):
                        for kt in range(KT):
                            for wi, xi in ((0, 0), (1, 0), (0, 1)):
                                last = mm(bk[:], w[wi][:, kt, it * P:(it + 1) * P], x[xi][:, kt, :],
                                          start=(kt == 0 and wi + xi == 0), stop=(kt == KT - 1 and xi == 1))
                            if other is not None and (w is g and kt == 2 or w is u and kt in (0, 2)):
                                next(other, None)
                    last.then_inc(s["gu_done"], 1)

            def down(inter, tiles, w, added, after=None):
                for b in range(B):
                    if added > 0 or b >= 2:
                        pe.wait_ge(s["x_added"], added + b - 1)
                    for it in range(tiles):
                        if b == 0 and (it == 0 or it >= tiles - 3):
                            pe.wait_ge(s["inter_done"], inter - tiles + max(it + 1, tiles - 3))
                        for ii, wi in ((0, 0), (0, 1), (1, 0)):
                            last = mm(bank[6 + b % 2][:], i_part[ii][:, it, b * CL:(b + 1) * CL], w[wi][:, it, :],
                                      start=(it == 0 and ii + wi == 0), stop=(it == tiles - 1 and ii == 1))
                    last.then_inc(s["down_done"], 1)
                    if after is not None:
                        after(b)

            def input_transposes(n, b):
                if b >= 2:
                    pe.wait_ge(s["xl_ready"], B * (n // B // 2) + b - 1)
                transposes(n)

            def gates_input(c, b):
                k = c * B + b
                transposes(4 * B + k)
                yield
                pe.wait_ge(s["xT_ready"], 4 * B + k + 1)
                if c == 0 and b == 0:
                    pe.wait_ge(s["rec_in"], 48)
                    pe.wait_ge(s["x_added"], B)
                if b >= 2:
                    pe.wait_ge(s["rin_ready"], k - 1)
                for gp in range(2):
                    for kt in range(KT):
                        last = mm(bank[(6 if c == 0 else 2) + b % 2][:, gp * CL:(gp + 1) * CL], lys[:, kt, gp * P:(gp + 1) * P],
                                  xT_rec[k % 2][:, kt, :], start=(kt == 0), stop=(kt == KT - 1))
                last.then_inc(s["rec_done"], 1)
                yield

            def between():
                for b in range(B):
                    yield from gates_input(0, b)
                pe.wait_ge(s["setup_in"], 16 * SETUP)
                pe.wait_ge(s["scale_ready"], 1)
                pe.wait_ge(s["rin_ready"], B)
                mm(bank[7][0:KW, 0:J], convw[:], wafT[:], start=True, stop=True)
                for h in range(2):
                    mm(bank[7][h * J:(h + 1) * J, J:J + P], wahT[:], ctxT[:, h, :], start=True, stop=True)
                    mm(bank[7][:, J + P + h * J:J + P + (h + 1) * J], ctxT[:, h, :], lgyT[:], start=True, stop=True)
                    last = mm(bank[6][:, h * 256:(h + 1) * 256], ctxT[:, h, :], lgsT[:], start=True, stop=True)
                last.then_inc(s["setup_mm"], 1)
                yield
                pe.wait_ge(s["setup_cp"], 1)
                for hi in range(2):
                    for ho in range(2):
                        last = mm(bank[6][:, hi * P + ho * J:hi * P + ho * J + J], ker[:, hi - ho + 1, :], u_sb[:], start=True, stop=True)
                last.then_inc(s["setup_mm"], 1)
                yield

            pe.wait_ge(s["attn_in"], 16 * 3)
            for _ in chunk_steps(0, attention):
                pass
            input_transposes(2 * B - 1, B - 1)
            pe.wait_ge(s["low_ready"], 4)
            pe.wait_ge(s["low_odd"], 4)
            pe.wait_ge(s["xl_ready"], B)
            gate_up(0, IT0, wg, wu, x_part, other=chunk_steps(1, attention))
            pe.wait_ge(s["attn_done"], 2 * B)
            pe.wait_ge(s["low_ready"], 7)
            pe.wait_ge(s["low_odd"], 6)

            def next_input(b):
                if b < 2:
                    for j in (2 * b, 2 * b + 1):
                        input_transposes(3 * B + j, j)

            down(IT0, IT0, wd, 0, next_input)
            pe.wait_ge(s["xl_ready"], 2 * B)
            gate_up(IT0, IT0, wg, wu, x_part, other=between())
            pe.wait_ge(s["setup_cp"], 2)

            def last_gates(b):
                for j in ([b - 1] if b >= 1 else []) + ([b] if b == B - 1 else []):
                    for _ in gates_input(1, j):
                        pass

            down(2 * IT0, IT0, wd, B, last_gates)
            pe.wait_ge(s["setup_v"], 1)
            pe.wait_ge(s["mask_ready"], 1)
            pe.wait_ge(s["rin_ready"], 2 * B)
            pe.wait_ge(s["part_ready"], 5)
            pe.wait_ge(s["identb_ready"], 1)

            def masks():
                mm(bank[2][:, 0:T], bsel[:], maskb[:], start=True, stop=False, skip_group_check=True)
                mm(bank[3][:, 0:8], etl[:], etr[:], start=True, stop=False, skip_group_check=True)

            def context_part(par):
                for j in range(3):
                    mm(bank[par][:, 0:P], identb[:], enc3[:, j, :], start=(j == 0), stop=False, skip_group_check=True)

            masks()
            context_part(0)

            with pe.Fori(0, S // 2) as i:
                for par in range(2):
                    l = i * 2 + par
                    state_part = [(0, sh), (1, sh), (0, sl)]
                    for j, st in state_part:
                        pe.wait_ge(s["sl_ready" if st is sl else "sh_ready"], l + 1)
                        last = mm(bank[par][:, 0:P], was2[:, j, :], st[:].unsqueeze(2).broadcast_to([J, B, TH]),
                                  start=False, stop=(st is sl), skip_group_check=True)
                    last.then_inc(s["pre_done"], 1)
                    for gp in range(2):
                        for j, st in ((0, sh), (1, sh), (2, sh), (0, sl), (1, sl)):
                            last = mm(bank[6][:, 4 * gp:4 * gp + 4], lss3[:, j, gp * P:(gp + 1) * P], st[:],
                                      start=(j == 0 and st is sh), stop=(j == 1 and st is sl))
                    last.then_inc(s["sp_done"], 1)
                    pe.wait_ge(s["th_s"], l + 1)
                    for b in range(B):
                        for h in range(2):
                            last = mm(bank[2][b * TH:(b + 1) * TH, h * TH:(h + 1) * TH], vah[:, h, :], th_hi[:, b * TH:(b + 1) * TH],
                                      start=False, stop=True, skip_group_check=True)
                    last.then_inc(s["eb_done"], 1)
                    for j in range(2):
                        mm(bank[3][:, 0:8], th_hi, vae2[:, j, :], start=False, stop=False, skip_group_check=True)
                    pe.wait_ge(s["th_lo_ready"], l + 1)
                    mm(bank[3][:, 0:8], th_lo, vae2[:, 0, :], start=False, stop=True, skip_group_check=True).then_inc(s["et_done"], 1)
                    pe.wait_ge(s["eh_ready"], l + 1)

                    def gates(parts, e, first, final):
                        for gp in range(2):
                            for j in parts:
                                for h in range(2):
                                    ins = mm(bank[4][:, 4 * gp:4 * gp + 4], hg2[:, j, h, gp * P:(gp + 1) * P], e[:, 4 * h:4 * h + 4],
                                             start=(first and gp == 0 and j == 0 and h == 0), stop=final, skip_group_check=True)
                        return ins

                    gates((0, 1), eh, True, False)
                    for h in range(2):
                        mm(bank[5][:, 8:12], onesb[:], eh[:, 4 * h:4 * h + 4], start=(h == 0), stop=False, skip_group_check=True)
                    pe.wait_ge(s["el_ready"], l + 1)
                    for h in range(2):
                        last = mm(bank[5][:, 8:12], onesb[:], el[:, 4 * h:4 * h + 4], start=False, stop=True, skip_group_check=True)
                    last.then_inc(s["sum_done"], 1)
                    gates((0,), el, False, True).then_inc(s["hg_done"], 1)
                    for j in range(2):
                        mm(bank[7][:, 0:8], fwd[:, j, :], eh[:], start=(j == 0), stop=False)
                    mm(bank[7][:, 0:8], fwd[:, 0, :], el[:], start=False, stop=True).then_inc(s["ah_done"], 1)
                    masks()
                    context_part(1 - par)
                    for h in range(2):
                        pe.wait_ge(s[f"q{h}_ready"], l + 1)
                        mm(bank[1 - par][:, 0:P], uh[:, h, :], qv[:, h, :, :], start=False, stop=False, skip_group_check=True)

            pe.wait_ge(s["hist_done"], S)
            pe.wait_ge(s["kept"], S)
            pe.wait_ge(s["fin_in"], 48)
            pe.wait_ge(s["w1_in"], 96)

            def prelude(c):
                for h in range(2):
                    mm(bank[6][0:J, :], hy[:, h, :], ahist[:, c * CL:(c + 1) * CL, 4 * h:4 * h + 4], start=(h == 0), stop=False)
                mm(bank[6][0:J, :], lsyT[:], shist[:, c * CL:(c + 1) * CL, :], start=False, stop=True).then_inc(s["y_done"], 1)
                yield
                pe.wait_ge(s["u_ready"], c + 1)
                before = (2 + c) * B
                for b in range(B):
                    if b >= 2:
                        pe.wait_ge(s["x_added"], before + b - 1)
                    mm(bank[6 + (b + 1) % 2][:], uT[:, b, :], lyy, start=True, stop=True).then_inc(s["yy_done"], 1)
                    yield
                for b in range(B):
                    n = 6 * B + c * B + b
                    pe.wait_ge(s["ln_ready"], n + 1)
                    if b < 2:
                        pe.wait_ge(s["x_added"], before + 3 + b)
                    else:
                        pe.wait_ge(s["xT_ready"], n - 1)
                    for kt in range(KT):
                        last = nc.tensor.transpose(bank[6 + (b + 1) % 2][:, kt * P:(kt + 1) * P], xn[:, n % 2, kt * P:(kt + 1) * P], ident[:])
                    last.then_inc(s["tr_done"], 1)
                    yield
                pe.wait_ge(s["xT_ready"], 6 * B + (c + 1) * B)
                for b in range(B):
                    for kt in range(KT):
                        last = mm(bank[7][:, b * NE:(b + 1) * NE], xT[:, kt, b * CL:(b + 1) * CL], gwT[:, kt, :], start=(kt == 0), stop=(kt == KT - 1))
                last.then_inc(s["lg_done"], 1)
                yield
                pe.wait_ge(s["wsel_ready"], c + 1)
                for b in range(B):
                    last = nc.tensor.transpose(bank[6][0:NE, b * CL:(b + 1) * CL], wsel[:, 0, b, :], ident[:])
                last.then_inc(s["wt_done"], 1)
                yield

            for _ in prelude(0):
                pass
            pe.wait_ge(s["expert_ready"], 1)
            pe.wait_ge(s["split_done"], S // 2 - SPLIT0 + 1)
            for c in range(NCH):
                pe.wait_ge(s["wT_low_ready"], c + 1)
                pe.wait_ge(s["xl_ready"], (3 + c) * B)
                gate_up(2 * IT0 + c * IT1, IT1, w1g, w1u, x1_part[c], wT[c], prelude(1) if c == 0 else None)
                if c == 0:
                    pe.wait_ge(s["wT_low_ready"], 2)
                down(2 * IT0 + (c + 1) * IT1, IT1, w1d, (4 + c) * B)


def kernel(**inputs):
    import concourse.bacc as bacc
    from concourse.bass_utils import run_bass_kernel_spmd

    i = {k: np.asarray(v) for k, v in inputs.items()}
    ctx = i["ctx_1024"]
    perm = np.concatenate([np.arange(q * J, (q + 1) * J) for q in (1, 2, 0, 3)])
    kT = ctx.reshape(B, T, 8, HD).transpose(2, 3, 0, 1)
    krep = np.repeat(kT[:, None], 4, 1).reshape(KT, P, B, T).transpose(1, 0, 2, 3)
    arrays = {
        "x": i["x"], "ctx_1024": ctx, "mask_SxS2_ff0": i["mask_SxS2_ff0"], "krep": krep,
        "lens": i["_lenS2"].reshape(B, 1),
        "gate_qT": i["L0_ffn_gate_q"].T, "gate_sT": i["L0_ffn_gate_s"].T,
        "up_qT": i["L0_ffn_up_q"].T, "up_sT": i["L0_ffn_up_s"].T,
        "down_qT": i["L0_ffn_down_q"].T, "down_sT": i["L0_ffn_down_s"].T,
        "LysT": i["L1_xattn_L_ys"][perm].T, "LssT": i["L1_xattn_L_ss"][perm].T,
        "LgsT": i["L1_xattn_L_gs_w"][perm].T, "gsb2": i["L1_xattn_L_gs_b"][perm].reshape(2, P).T,
        "LgyT": i["L1_xattn_L_gy_w"].T, "LsyT": i["L1_xattn_L_sy"].T, "bgy": i["L1_xattn_L_gy_b"].reshape(J, 1),
        "LyyT": i["L1_xattn_L_yy_w"].T, "byy": i["L1_xattn_L_yy_b"].reshape(1, H),
        "ctxT": ctx.reshape(B, 2, TH, D).transpose(3, 1, 0, 2).reshape(D, 2, P),
        "WahT": i["L1_xattn_Wa_h"].T, "WasT": i["L1_xattn_Wa_s"].T, "WafT": i["L1_xattn_Wa_f"].T,
        "convw": i["L1_xattn_conv_w"].reshape(FCH, KW), "ba": i["L1_xattn_ba"].reshape(J, 1), "va": i["L1_xattn_va"].reshape(J, 1),
        "gwT": i["L1_ffn_gate_w"].T, "g1T": i["L1_ffn_g"].T, "u1T": i["L1_ffn_u"].T, "d1T": i["L1_ffn_d"].T,
        **shape_constants(),
    }
    arrays = {"d_" + k: np.ascontiguousarray(v) for k, v in arrays.items()}
    nc = bacc.Bacc("TRN2", target_bir_lowering=False, num_devices=1)
    aps = {k[2:]: nc.dram_tensor(k, v.shape, mybir.dt.from_np(v.dtype), kind="ExternalInput").ap() for k, v in arrays.items()}
    out = nc.dram_tensor("d_out", (B, S, H), F32, kind="ExternalOutput").ap()
    build(nc, aps, out)
    r = run_bass_kernel_spmd(nc, [arrays], core_ids=[0])
    return r.results[0]["d_out"]
```
